# Optimizing a Trainium2 kernel written in Bass

```python
import numpy as np
import jax
import jax.numpy as jnp

def _softmax(x, axis=-1):
    return jax.nn.softmax(x, axis=axis)

def _gelu(x):
    return jax.nn.gelu(x, approximate=True)

def _silu(x):
    return jax.nn.silu(x)

def _sigmoid(x):
    return jax.nn.sigmoid(x)

def _layernorm(x, axis=-1, eps=1e-05):
    m = jnp.mean(x, axis=axis, keepdims=True)
    v = jnp.var(x, axis=axis, keepdims=True)
    return (x - m) / jnp.sqrt(v + eps)

def _scatter_add(tgt, idx, src, axis=0):
    return tgt.at[idx].add(src)

def _segment_sum(src, seg, n):
    return jax.ops.segment_sum(src, seg, n)
kernel_name = 'mk_decoder_postln_d1_seqx_r8_723cc0'

def setup_inputs(seed: int=0):
    np.random.seed(seed)
    _w = jnp.asarray

    def _rec_inputs():
        import jax
        import jax.numpy as jnp
        _rk = jax.random.key(seed)
        x = -0.0003929 + 0.9999 * jax.random.normal(jax.random.fold_in(_rk, 1), (4, 256, 512), jnp.float32)
        _lenS = 256 - jax.random.randint(jax.random.fold_in(_rk, 7), (4,), 0, max(1, 256 // 4) + 1, jnp.int32)
        _lenS2 = 64 - jax.random.randint(jax.random.fold_in(_rk, 8), (4,), 0, max(1, 64 // 4) + 1, jnp.int32)
        _ctx_4096P = jax.random.normal(jax.random.fold_in(_rk, 11), (4, 16, 512), jnp.float32)
        _ctx_4096c = jax.random.dirichlet(jax.random.fold_in(_rk, 511), 0.3 * jnp.ones((16,), jnp.float32), (4, 64))
        _ctx_4096t = jnp.einsum('bsk,bkd->bsd', _ctx_4096c, _ctx_4096P)
        _ctx_4096t = _ctx_4096t * jax.lax.rsqrt(jnp.mean(jnp.square(_ctx_4096t)) + 1e-12) * 0.953939
        ctx_4096 = 2.81802e-05 + 1.00001 * (_ctx_4096t + 0.3 * jax.random.normal(jax.random.fold_in(_rk, 611), (4, 64, 512), jnp.float32))
        _validS = jnp.arange(256)[None, :] < _lenS[:, None]
        _validS2 = jnp.arange(64)[None, :] < _lenS2[:, None]
        _causal = jnp.tril(jnp.ones((256, 256), dtype=bool))
        mask_BxSxS2_ff0 = jnp.where(jnp.ones((4, 256, 64), dtype=bool), 0.0, -1000000000.0).astype(jnp.float32)
        return (x, ctx_4096, mask_BxSxS2_ff0)
    x, ctx_4096, mask_BxSxS2_ff0 = _rec_inputs()

    def _L0_attn_setup():
        import math
        import jax, jax.numpy as jnp
        import numpy as np
        IN_F, OUT_F, HID = (512, 512, 512)
        WINDOW, STRIPES = (6, 3)

        def make_sparse_mask(n_in=IN_F, n_out=OUT_F, window=WINDOW, stripes=STRIPES):
            m = np.zeros((n_in, n_out), dtype=np.float32)
            stride = int(math.sqrt(n_in))
            for k in range(stripes):
                ps = stride * k
                for i in range(0, n_in, window):
                    m[ps + i:ps + i + window, i:i + window] = 1.0
            mb = m.astype(bool)
            return jnp.asarray((mb | mb.T).astype(np.float32))
        key = jax.random.key(seed)
        k1, k2, k3, k4 = jax.random.split(key, 4)
        scale = 1.0 / math.sqrt(IN_F)
        x = jax.random.normal(k1, (8, 96, IN_F), dtype=jnp.float32)
        w1 = jax.random.normal(k2, (HID, IN_F), dtype=jnp.float32) * scale
        w2 = jax.random.normal(k3, (OUT_F, HID), dtype=jnp.float32) * scale
        b2 = jax.random.normal(k4, (OUT_F,), dtype=jnp.float32) * scale
        return {'x': x, 'w1': w1, 'w2': w2, 'b2': b2, 'sparse_mask': make_sparse_mask()}
    _L0_attn_all = _L0_attn_setup()
    _L0_attn_in = {k: v for k, v in _L0_attn_all.items() if k in ('w1', 'w2', 'b2', 'sparse_mask')}
    del _L0_attn_all

    def _L0_xattn_setup():
        import jax, jax.numpy as jnp
        import numpy as np
        B, S, D = (4, 128, 512)
        HQ, HKV, DK, DV = (32, 8, 128, 128)

        def apply_rope(x, positions):
            d = x.shape[-1]
            inv_freq = 1.0 / 10000.0 ** (jnp.arange(0, d, 2, dtype=jnp.float32) / d)
            ang = positions.astype(jnp.float32)[:, None] * inv_freq[None, :]
            cos = jnp.cos(ang)[None, None]
            sin = jnp.sin(ang)[None, None]
            x1, x2 = (x[..., :d // 2], x[..., d // 2:])
            return jnp.concatenate([x1 * cos - x2 * sin, x2 * cos + x1 * sin], axis=-1)
        key = jax.random.key(seed)
        ks = jax.random.split(key, 8)
        return {'query': jax.random.normal(ks[0], (B, S, D), jnp.float32), 'key': jax.random.normal(ks[1], (B, S, D), jnp.float32), 'value': jax.random.normal(ks[2], (B, S, D), jnp.float32), 'mask': jnp.zeros((B, S, S), jnp.float32), 'wq': jax.random.normal(ks[3], (D, HQ * DK), jnp.float32) * 0.02, 'wk': jax.random.normal(ks[4], (D, HKV * DK), jnp.float32) * 0.02, 'wv': jax.random.normal(ks[5], (D, HKV * DV), jnp.float32) * 0.02, 'wo': jax.random.normal(ks[6], (HQ * DV, D), jnp.float32) * 0.02, 'curr_seq_pos': 0}
    _L0_xattn_all = _L0_xattn_setup()
    _L0_xattn_in = {k: v for k, v in _L0_xattn_all.items() if k in ('wq', 'wk', 'wv', 'wo')}
    del _L0_xattn_all

    def _L0_ffn_setup():
        import jax, jax.numpy as jnp
        import numpy as np
        IMAGE_START_POS = 34
        Q_START = IMAGE_START_POS + 72 + 1
        Q_END = -1
        LORA_ALPHA = 32
        LORA_RANK = 16
        SCALING = LORA_ALPHA / LORA_RANK
        key = jax.random.key(seed)
        ks = jax.random.split(key, 7)
        B_, S, D, O, E, R = (4, 256, 512, 512, 8, LORA_RANK)
        s = 0.02
        return {'x': jax.random.normal(ks[0], (B_, S, D), jnp.float32), 'W': jax.random.normal(ks[1], (O, D), jnp.float32) * s, 'b': jax.random.normal(ks[2], (O,), jnp.float32) * s, 'A': jax.random.normal(ks[3], (E, R, D), jnp.float32) * s, 'B': jax.random.normal(ks[4], (E, O, R), jnp.float32) * s, 'router_W': jax.random.normal(ks[5], (E, D), jnp.float32) * s, 'router_b': jax.random.normal(ks[6], (E,), jnp.float32) * s}
    _L0_ffn_all = _L0_ffn_setup()
    _L0_ffn_in = {k: v for k, v in _L0_ffn_all.items() if k in ('W', 'b', 'A', 'B', 'router_W', 'router_b')}
    del _L0_ffn_all
    return {'x': x, 'ctx_4096': ctx_4096, 'mask_BxSxS2_ff0': mask_BxSxS2_ff0, 'L0_attn_w1': _L0_attn_in['w1'], 'L0_attn_w2': _L0_attn_in['w2'], 'L0_attn_b2': _L0_attn_in['b2'], 'L0_attn_sparse_mask': _L0_attn_in['sparse_mask'], 'L0_xattn_wq': _L0_xattn_in['wq'], 'L0_xattn_wk': _L0_xattn_in['wk'], 'L0_xattn_wv': _L0_xattn_in['wv'], 'L0_xattn_wo': _L0_xattn_in['wo'], 'L0_ffn_W': _L0_ffn_in['W'], 'L0_ffn_b': _L0_ffn_in['b'], 'L0_ffn_A': _L0_ffn_in['A'], 'L0_ffn_B': _L0_ffn_in['B'], 'L0_ffn_router_W': _L0_ffn_in['router_W'], 'L0_ffn_router_b': _L0_ffn_in['router_b']}

def reference(x, ctx_4096, mask_BxSxS2_ff0, L0_attn_w1, L0_attn_w2, L0_attn_b2, L0_attn_sparse_mask, L0_xattn_wq, L0_xattn_wk, L0_xattn_wv, L0_xattn_wo, L0_ffn_W, L0_ffn_b, L0_ffn_A, L0_ffn_B, L0_ffn_router_W, L0_ffn_router_b):
    import jax
    import jax.numpy as jnp

    def _L0_attn_ref(x, w1, w2, b2, sparse_mask):
        import math
        import jax, jax.numpy as jnp
        import numpy as np
        IN_F, OUT_F, HID = (512, 512, 512)
        WINDOW, STRIPES = (6, 3)

        def make_sparse_mask(n_in=IN_F, n_out=OUT_F, window=WINDOW, stripes=STRIPES):
            m = np.zeros((n_in, n_out), dtype=np.float32)
            stride = int(math.sqrt(n_in))
            for k in range(stripes):
                ps = stride * k
                for i in range(0, n_in, window):
                    m[ps + i:ps + i + window, i:i + window] = 1.0
            mb = m.astype(bool)
            return jnp.asarray((mb | mb.T).astype(np.float32))
        attn = jnp.einsum('ds,td->st', w1, w2) * sparse_mask
        y = jnp.einsum('bds,st->bdt', x, attn) + b2
        return jax.nn.gelu(y, approximate=False)

    def _L0_xattn_ref(query, key, value, mask, wq, wk, wv, wo, curr_seq_pos):
        import jax, jax.numpy as jnp
        import numpy as np
        B, S, D = (4, 128, 512)
        HQ, HKV, DK, DV = (32, 8, 128, 128)

        def apply_rope(x, positions):
            d = x.shape[-1]
            inv_freq = 1.0 / 10000.0 ** (jnp.arange(0, d, 2, dtype=jnp.float32) / d)
            ang = positions.astype(jnp.float32)[:, None] * inv_freq[None, :]
            cos = jnp.cos(ang)[None, None]
            sin = jnp.sin(ang)[None, None]
            x1, x2 = (x[..., :d // 2], x[..., d // 2:])
            return jnp.concatenate([x1 * cos - x2 * sin, x2 * cos + x1 * sin], axis=-1)
        bs, sq, _ = query.shape
        sk = key.shape[1]
        n_groups = HQ // HKV
        q = (query @ wq).reshape(bs, sq, HQ, DK).transpose(0, 2, 1, 3)
        k = (key @ wk).reshape(bs, sk, HKV, DK)
        v = (value @ wv).reshape(bs, sk, HKV, DV)
        k = jnp.repeat(k, n_groups, axis=2).transpose(0, 2, 1, 3)
        v = jnp.repeat(v, n_groups, axis=2).transpose(0, 2, 1, 3)
        scale = jnp.sqrt(jnp.float32(DK))
        pos = curr_seq_pos + jnp.arange(sq)
        q = apply_rope(q, pos)
        k = apply_rope(k, curr_seq_pos + jnp.arange(sk))
        scores = jnp.einsum('bhqd,bhkd->bhqk', q, k) / scale
        m = jax.lax.dynamic_slice(mask, (0, curr_seq_pos, 0), (bs, sq, sk))
        attn = jax.nn.softmax(scores + m[:, None, :, :], axis=-1)
        out = jnp.einsum('bhqk,bhkd->bhqd', attn, v)
        out = out.transpose(0, 2, 1, 3).reshape(bs, sq, HQ * DV)
        return out @ wo

    def _L0_ffn_ref(x, W, b, A, B, router_W, router_b):
        import jax, jax.numpy as jnp
        import numpy as np
        IMAGE_START_POS = 34
        Q_START = IMAGE_START_POS + 72 + 1
        Q_END = -1
        LORA_ALPHA = 32
        LORA_RANK = 16
        SCALING = LORA_ALPHA / LORA_RANK
        x_q = x[:, Q_START:Q_END, :]
        q = x_q.mean(axis=1)
        logits = q @ router_W.T + router_b
        routing = jax.nn.softmax(logits, axis=-1)
        base = x @ W.T + b
        t = jnp.einsum('bsd,erd->bser', x, A)
        lora = jnp.einsum('bser,eor,be->bso', t, B, routing) * SCALING
        return base + lora
    x = _layernorm(x + _L0_attn_ref(x, L0_attn_w1, L0_attn_w2, L0_attn_b2, L0_attn_sparse_mask), axis=-1)
    x = _layernorm(x + _L0_xattn_ref(x, ctx_4096, ctx_4096, mask_BxSxS2_ff0, L0_xattn_wq, L0_xattn_wk, L0_xattn_wv, L0_xattn_wo, 0), axis=-1)
    x = _layernorm(x + _L0_ffn_ref(x, L0_ffn_W, L0_ffn_b, L0_ffn_A, L0_ffn_B, L0_ffn_router_W, L0_ffn_router_b), axis=-1)
    return x

_drawn_inputs = setup_inputs


def setup_inputs(seed=0):
    import zlib

    import numpy as np

    out = dict(_drawn_inputs(seed))
    spreads = {}
    factors = {'L0_attn_b2': 2.768,
     'L0_xattn_wq': 3.007,
     'L0_xattn_wk': 3.011,
     'L0_ffn_b': 3.228,
     'L0_ffn_router_W': 21.442,
     'L0_ffn_router_b': 200.0}
    for name, (base, spread) in spreads.items():
        noise = np.random.default_rng([zlib.crc32(name.encode()), seed]).standard_normal(out[name].shape)
        drawn = base * np.exp(spread * noise) if base else spread * noise
        out[name] = jnp.asarray(drawn.astype(out[name].dtype))
    for name, factor in factors.items():
        out[name] = (out[name] * factor).astype(out[name].dtype)
    return out
```

```python
from contextlib import ExitStack
import math

import numpy as np

import concourse.bass as bass
from concourse import mybir

F32 = mybir.dt.float32
F32R = mybir.dt.float32r
I32 = mybir.dt.int32
ACT = mybir.ActivationFunctionType
ALU = mybir.AluOpType
AX_X = mybir.AxisListType.X

P = 128
LN_EPS = 1e-5
RSQRT_GUESS = float(0x5F3759DF)
NEWTON_STEPS = 3
ROUTE_FROM, ROUTE_END = 107, -1
LORA_SCALING = 2.0


def rope_tables(dk, positions):
    inv_freq = (1.0 / np.float32(10000.0) ** (np.arange(0, dk, 2, dtype=np.float32) / np.float32(dk))).astype(np.float32)
    ang = inv_freq[:, None] * np.arange(positions, dtype=np.float32)[None, :]
    cos, sin = np.cos(ang), np.sin(ang)
    return np.stack([np.concatenate([cos, cos]), np.concatenate([-sin, sin])]).astype(np.float32)


def route_weights(tokens):
    w = np.zeros(tokens, np.float32)
    w[ROUTE_FROM:ROUTE_END] = 1.0
    w /= w.sum()
    return np.ascontiguousarray(w.reshape(-1, P).T)


def decoder_layer(nc, x, ctx_in, amask, w1, w2, b2, smask, wq, wk, wv, wo, fW, fb, fA, fB, rW, rb, rope, route, out):
    B, S, D = x.shape
    KS = ctx_in.shape[1]
    HQ, DK = wq.shape[1] // P, P
    HKV = wk.shape[1] // P
    G = HQ // HKV
    E, R = fA.shape[0], fA.shape[1]
    C = D // P
    NT = B * S // P
    TPB = S // P
    HALF = 512
    assert (B, S, D, KS, G, E * R) == (4, 256, 512, 64, 4, 128)

    x_v = x.rearrange("b s d -> (b s) d").rearrange("(t p) d -> p t d", p=P)
    out_v = out.rearrange("b s d -> (b s) d").rearrange("(t p) d -> p t d", p=P)
    amask_v = amask.rearrange("b s k -> (b s) k").rearrange("(t p) k -> p t k", p=P)
    ctx_v = ctx_in.rearrange("b s d -> (b s) d").rearrange("(t p) d -> p t d", p=P)

    def rows(a):
        return a.rearrange("(c p) n -> p c n", p=P)

    with ExitStack() as es:
        def sb(name, shape, dt=F32):
            return es.enter_context(nc.sbuf_tensor(name, shape, dt))

        def sem(name):
            return es.enter_context(nc.semaphore(name))

        X = sb("X", [P, NT, D])
        XTh, XTl = (sb(f"XT{s}", [P, C, B * S], F32R) for s in "hl")
        VWh, VWl = (sb(f"VW{s}", [P, 2, B, D], F32R) for s in "hl")
        VWr = sb("VWr", [P, 2, 2, D])
        WQr = sb("WQr", [P, C, G * DK])
        WQh, WQl = (sb(f"WQ{s}", [P, C, G * DK], F32R) for s in "hl")
        WOr = sb("WOr", [P, G, D])
        WOh, WOl = (sb(f"WO{s}", [P, G, D], F32R) for s in "hl")
        KVr = sb("KVr", [P, 2, C, DK])
        KVh, KVl = (sb(f"KV{s}", [P, 2, C, DK], F32R) for s in "hl")
        CTh, CTl = (sb(f"CT{s}", [P, C, B * KS], F32R) for s in "hl")
        KR = sb("KR", [P, 2, 3, KS])
        KSW = sb("KSW", [P, B * KS])
        KA = sb("KA", [P, B * KS])
        VTh, VTl = (sb(f"VT{s}", [P, B * KS], F32R) for s in "hl")
        QR = sb("QR", [P, 2, B * S])
        QS = sb("QS", [P, 2, HALF])
        QA = sb("QA", [P, 2, HALF])
        PB = sb("PB", [P, NT, 2, KS])
        SM = sb("SM", [P, 2, NT * KS])
        PTh, PTl = (sb(f"PT{s}", [P, 2, B * S], F32R) for s in "hl")
        MSK = sb("MSK", [P, NT, KS])
        COS = sb("COS", [P, S])
        SIN = sb("SIN", [P, S])
        ID = sb("ID", [P, P])
        MX = sb("MX", [P, 2, NT])
        SU = sb("SU", [P, 2, NT])
        RI = sb("RI", [P, 2, NT])
        BST = sb("BST", [P, 2, 6])
        MV = sb("MV", [P, NT, 2])
        VE = sb("VE", [P, NT])
        RS = sb("RS", [P, NT])
        NW = sb("NW", [P, NT])
        VH = sb("VH", [P, NT])
        RTE = sb("RTE", [P, TPB])
        QT = sb("QT", [P, C, B])
        RWT = sb("RWT", [P, C, E])
        RB = sb("RB", [B, E])
        LG = sb("LG", [B, 4, E])
        LS = sb("LS", [B, 4])
        R2 = sb("R2", [B, E * R])
        RT = sb("RT", [P, B])

        bank = es.enter_context(nc.psum_tensor("bank", [P, 8, 512], F32))
        Q_BANK, S_BANK, T_BANK, VW_BANK, PV_BANK = 0, 2, 4, 5, 6

        names = """w2_in w1_in mask_in ctx_in_ b2_in rope_in wq_in wo_in wk_in wv_in fw_in fa_in fbm_in rw_in rb_in
        fb_in route_in amask_in stored ident ones_set w2t_mm w2t_hi w2t_lo w1_hi w1_lo b2_hi b2_lo tr_mm tr_hi tr_lo
        at_mm at_masked at_hi at_lo y_mm gelu_done x_added ln_stats ln_mean ln_guess ln_newton ln_out
        wq_hi wq_lo wo_hi wo_lo wkv_hi wkv_lo kv_mm kv_act k_cos k_sin k_rot v_lo
        q_mm q_swap q_cos q_sin q_rot s_mm s_masked s_max s_sub s_exp s_sum s_inv p_done
        t_mm pt_hi pt_lo vw_mm vw_raw vw_hi vw_lo pv_mm
        f_mm f_hi f_lo mean_mm mean_out lg_mm lg_step lg_exp r_out rt_mm rt_out tt_mm ts_out ts_hi ts_lo
        fy_mm fy_out bias_in""".split()
        sm = {n: sem(n) for n in names}
        x_in = [sem(f"x_in{i}") for i in range(4)]

        def need(eng, name, value):
            if not isinstance(value, int) or value > 0:
                eng.wait_ge(sm[name], value)

        block = es.enter_context(nc.Block())
        f32 = lambda ap: ap.bitcast(F32)

        def y_bank(t):
            return 2 + t % 2

        def fy_bank(t):
            return (6, 7, 2, 3)[t % 4]

        F_BANKS = (5, 0, 1, 5, 0, 1, 5)
        LAST = HKV - 1

        @block.sync
        def _(sp):
            def load(dst, src, name):
                sp.dma_start(dst, src).then_inc(sm[name], 16)

            load(WQr[:, :, :], rows(w2), "w2_in")
            load(WOr[:, :, :], rows(w1), "w1_in")
            load(QR[:, :, 0:D], ctx_v, "ctx_in_")
            for i in range(4):
                sp.dma_start(X[:, 2 * i:2 * i + 2, :], x_v[:, 2 * i:2 * i + 2, :]).then_inc(x_in[i], 16)
                if i == 0:
                    load(VWr[:, :, :, :].rearrange("p a b n -> p (a b) n"), rows(smask), "mask_in")
                    load(QS[0:1, 0, :], b2.rearrange("(a n) -> a n", a=1), "b2_in")
            load(KVr[:, 0, :, :], rows(wk)[:, :, 0:DK], "wk_in")
            load(KVr[:, 1, :, :], rows(wv)[:, :, 0:DK], "wv_in")
            load(COS[:, :], rope[0, :, :], "rope_in")
            load(SIN[:, :], rope[1, :, :], "rope_in")
            load(MSK[:, :, :], amask_v, "amask_in")
            load(RTE[:, :], route, "route_in")
            load(RB[:, :], rb.rearrange("(a n) -> a n", a=1).broadcast_to([B, E]), "rb_in")
            sp.wait_ge(sm["w2t_mm"], C)
            load(WQr[:, :, :], rows(wq)[:, :, 0:G * DK], "wq_in")
            sp.wait_ge(sm["w1_lo"], 1)
            load(WOr[:, :, :], rows(wo[0:G * DK, :]), "wo_in")
            with sp.Fori(1, HKV) as g:
                kv_at, q_at = sp.snap(g * DK), sp.snap(g * G * DK)
                need(sp, "wkv_lo", 2 * g)
                load(KVr[:, 0, :, :], rows(wk)[:, :, bass.ds(kv_at, DK)], "wk_in")
                load(KVr[:, 1, :, :], rows(wv)[:, :, bass.ds(kv_at, DK)], "wv_in")
                need(sp, "wq_lo", g * G)
                load(WQr[:, :, :], rows(wq)[:, :, bass.ds(q_at, G * DK)], "wq_in")
                need(sp, "wo_lo", g * G)
                load(WOr[:, :, :], rows(wo[bass.ds(q_at, G * DK), :]), "wo_in")
            need(sp, "wq_lo", HKV * G)
            load(WQr[:, :, :], rows(fW), "fw_in")
            need(sp, "wo_lo", HKV * G)
            load(WOr[:, 0, :], fA.rearrange("e r d -> (e r) d"), "fa_in")
            for oc in range(C):
                load(WOr[:, 1, oc * P:(oc + 1) * P].rearrange("p (e r) -> p e r", e=E),
                     fB[:, oc * P:(oc + 1) * P, :].rearrange("e p r -> p e r"), "fbm_in")
            load(WOr[0:E, 2, :], rW, "rw_in")
            load(WOr[:, 3, :], fb.rearrange("(a n) -> a n", a=1).broadcast_to([P, D]), "fb_in")
            for t in range(NT):
                sp.wait_ge(sm["ln_out"], 2 * NT + t + 1)
                load(out_v[:, t, :], X[:, t, :], "stored")
            sp.wait_ge(sm["stored"], 16 * NT)

        @block.tensor
        def _(pe):
            def mm3(o, lh, ll, rh, rl, start=True, stop=True):
                pe.matmul(o, lh, rh, start=start, stop=False)
                pe.matmul(o, lh, rl, start=False, stop=False)
                return pe.matmul(o, ll, rh, start=False, stop=stop)

            def transpose_tile(n, tiles):
                need(pe, "tr_lo", n - 1)
                for out_at, src in tiles:
                    m = pe.transpose(bank[:, PV_BANK + n % 2, out_at:out_at + P], src, ID[:, :])
                m.then_inc(sm["tr_mm"], 1)

            def x_tile(n, t):
                transpose_tile(n, [(c * P, X[:, t, c * P:(c + 1) * P]) for c in range(C)])

            def attn_weights(s):
                for c in range(C):
                    m = mm3(bank[:, (4, 5, 0, 1)[s], :], WOh[:, c, s * P:(s + 1) * P], WOl[:, c, s * P:(s + 1) * P],
                            WQh[:, c, :], WQl[:, c, :], start=c == 0, stop=c == C - 1)
                m.then_inc(sm["at_mm"], 1)

            def dense(t):
                need(pe, "tr_lo", 3 + t)
                need(pe, "gelu_done", t - 1)
                o = bank[:, y_bank(t), :]
                pe.matmul(o, PTh[0:1, 1, 0:P], PTh[0:1, 0, 0:D], start=True, stop=False)
                pe.matmul(o, PTh[0:1, 1, 0:P], PTl[0:1, 0, 0:D], start=False, stop=False)
                for s in range(C):
                    m = mm3(o, XTh[:, s, t * P:(t + 1) * P], XTl[:, s, t * P:(t + 1) * P],
                            VWh[:, 0, s, :], VWl[:, 0, s, :], start=False, stop=s == C - 1)
                m.then_inc(sm["y_mm"], 1)

            def keys(g):
                need(pe, "wkv_lo", 2 * g + 1)
                need(pe, "vw_raw", 2 * G * g)
                for c in range(C):
                    mm3(bank[:, VW_BANK, 0:B * KS], KVh[:, 0, c, :], KVl[:, 0, c, :], CTh[:, c, :], CTl[:, c, :],
                        start=c == 0, stop=c == C - 1)

            def values(g):
                need(pe, "wkv_lo", 2 * g + 2)
                for c in range(C):
                    m = mm3(bank[:, VW_BANK, B * KS:2 * B * KS], KVh[:, 1, c, :], KVl[:, 1, c, :],
                            CTh[:, c, :], CTl[:, c, :], start=c == 0, stop=c == C - 1)
                m.then_inc(sm["kv_mm"], 1)

            def query(g, h, half):
                need(pe, "wq_lo", G * g + h + 1)
                need(pe, "q_cos", 2 * G * g + 2 * h + half - 1)
                for c in range(C):
                    m = mm3(bank[:, Q_BANK + half, :], WQh[:, c, h * DK:(h + 1) * DK], WQl[:, c, h * DK:(h + 1) * DK],
                            XTh[:, c, half * HALF:(half + 1) * HALF], XTl[:, c, half * HALF:(half + 1) * HALF],
                            start=c == 0, stop=c == C - 1)
                m.then_inc(sm["q_mm"], 1)

            def scores(g, h):
                need(pe, "q_rot", 2 * G * g + 2 * h + 2)
                need(pe, "k_rot", g + 1)
                need(pe, "s_masked", G * g + h)
                for t in range(NT):
                    b = t // TPB
                    m = pe.matmul(bank[:, S_BANK + t // 4, t % 4 * P:(t % 4 + 1) * P], QR[:, h % 2, t * P:(t + 1) * P],
                                  KR[:, b // 2, b % 2:b % 2 + 2, :].rearrange("p b k -> p (b k)"), start=True, stop=True)
                m.then_inc(sm["s_mm"], 1)

            def probs_transpose(g, pair, part):
                need(pe, "p_done", G * g + 2 * pair + 2)
                need(pe, "pt_lo", 4 * g + 2 * pair + part)
                for j in range(4):
                    m = pe.transpose(bank[:, T_BANK, j * P:(j + 1) * P],
                                     PB[:, 4 * part + j, :, :].rearrange("p a k -> p (a k)"), ID[:, :])
                m.then_inc(sm["t_mm"], 1)

            def value_out(g, u):
                pair, par, bp = u // 4, u // 2 % 2, u % 2
                h = 2 * pair + par
                need(pe, "wo_lo", G * g + h + 1)
                need(pe, "v_lo", g + 1)
                need(pe, "vw_raw", 2 * G * g + u)
                mm3(bank[:, VW_BANK, :], VTh[:, bp * P:(bp + 1) * P], VTl[:, bp * P:(bp + 1) * P],
                    WOh[:, h, :], WOl[:, h, :]).then_inc(sm["vw_mm"], 1)

            def attend(g, t):
                need(pe, "pt_lo", 4 * g + 2 + t // 4 + 1)
                need(pe, "vw_lo", 4 * g + 4)
                need(pe, "x_added", NT + NT * g + t - 1)
                for pair in range(2):
                    m = mm3(bank[:, PV_BANK + t % 2, :], PTh[:, pair, t * P:(t + 1) * P], PTl[:, pair, t * P:(t + 1) * P],
                            VWh[:, pair, t // TPB, :], VWl[:, pair, t // TPB, :], start=pair == 0, stop=pair == 1)
                m.then_inc(sm["pv_mm"], 1)

            def group(g, first=False):
                if first:
                    keys(g)
                    values(g)
                    need(pe, "tr_lo", 14)
                    query(g, 0, 0)
                    for t in range(4, NT):
                        need(pe, "ln_out", t + 1)
                        x_tile(10 + t, t)
                    need(pe, "tr_lo", 18)
                    query(g, 0, 1)
                else:
                    scores(g - 1, 3)
                    query(g, 0, 0)
                    query(g, 0, 1)
                    keys(g)
                    probs_transpose(g - 1, 1, 0)
                    values(g)
                    probs_transpose(g - 1, 1, 1)
                    for t in range(NT):
                        attend(g - 1, t)
                query(g, 1, 0)
                value_out(g, 0)
                query(g, 1, 1)
                value_out(g, 1)
                scores(g, 0)
                query(g, 2, 0)
                value_out(g, 2)
                query(g, 2, 1)
                value_out(g, 3)
                scores(g, 1)
                value_out(g, 4)
                query(g, 3, 0)
                value_out(g, 5)
                query(g, 3, 1)
                value_out(g, 6)
                probs_transpose(g, 0, 0)
                scores(g, 2)
                probs_transpose(g, 0, 1)
                value_out(g, 7)

            need(pe, "ident", 2)
            pe.wait_ge(sm["w2_in"], 16)
            for c in range(C):
                for t in range(C):
                    m = pe.transpose(bank[:, c, t * P:(t + 1) * P], WQr[:, t, c * P:(c + 1) * P], ID[:, :])
                m.then_inc(sm["w2t_mm"], 1)
            pe.wait_ge(sm["ctx_in_"], 16)
            for n in range(2):
                transpose_tile(n, [(256 * j + r * P, QR[:, r, (2 * n + j) * P:(2 * n + j + 1) * P])
                                   for j in range(2) for r in range(2)])
            pe.wait_ge(x_in[0], 16)
            x_tile(2, 0)
            x_tile(3, 1)
            need(pe, "w2t_lo", C)
            need(pe, "w1_lo", 1)
            for s in range(C):
                attn_weights(s)
                if s in (0, 2):
                    pe.wait_ge(x_in[1 + s // 2], 16)
                x_tile(4 + s, 2 + s)
            need(pe, "at_lo", C)
            need(pe, "b2_lo", 1)
            dense(0)
            pe.wait_ge(x_in[3], 16)
            x_tile(8, 6)
            dense(1)
            x_tile(9, 7)
            dense(2)
            dense(3)
            dense(4)
            need(pe, "ln_out", 2)
            x_tile(10, 0)
            x_tile(11, 1)
            dense(5)
            dense(6)
            need(pe, "ln_out", 4)
            x_tile(12, 2)
            x_tile(13, 3)
            dense(7)

            group(0, first=True)
            with pe.Fori(1, HKV) as g:
                group(g)

            scores(LAST, 3)
            need(pe, "vw_raw", 2 * G * HKV)
            need(pe, "q_cos", 2 * G * HKV)
            pe.wait_ge(sm["fw_in"], 16)
            for j in range(7):
                if j >= 3:
                    need(pe, "f_lo", j - 2)
                o = bank[:, F_BANKS[j], :]
                if j == 4:
                    pe.wait_ge(sm["fa_in"], 16)
                if j == 5:
                    pe.wait_ge(sm["fbm_in"], 16 * C)
                if j == 6:
                    pe.wait_ge(sm["rw_in"], 16)
                for t in range(C):
                    if j < 4:
                        src = WQr[:, t, j * P:(j + 1) * P]
                    else:
                        src = WOr[:, j - 4, t * P:(t + 1) * P]
                    if j == 6:
                        m = pe.transpose(o[:, t * E:(t + 1) * E], src[0:E, :], ID[0:E, 0:E])
                    else:
                        m = pe.transpose(o[:, t * P:(t + 1) * P], src, ID[:, :])
                m.then_inc(sm["f_mm"], 1)
            probs_transpose(LAST, 1, 0)
            probs_transpose(LAST, 1, 1)
            for t in range(NT):
                attend(LAST, t)

            def mean(b):
                for c in range(C):
                    for i in range(TPB):
                        m = pe.matmul(bank[:, 1, c * B + b:c * B + b + 1], X[:, TPB * b + i, c * P:(c + 1) * P],
                                      RTE[:, i:i + 1], start=i == 0, stop=i == TPB - 1)
                return m

            def lora_in(half):
                need(pe, "tr_lo", 18 + 4 * (half + 1))
                for c in range(C):
                    m = mm3(bank[:, (5, 0)[half], :], WOh[:, 0, c * P:(c + 1) * P], WOl[:, 0, c * P:(c + 1) * P],
                            XTh[:, c, half * HALF:(half + 1) * HALF], XTl[:, c, half * HALF:(half + 1) * HALF],
                            start=c == 0, stop=c == C - 1)
                m.then_inc(sm["tt_mm"], 1)

            def base(t):
                if t >= 4:
                    need(pe, "fy_out", t - 3)
                need(pe, "tr_lo", 18 + t + 1)
                for c in range(C):
                    mm3(bank[:, fy_bank(t), :], XTh[:, c, t * P:(t + 1) * P], XTl[:, c, t * P:(t + 1) * P],
                        WQh[:, c, :], WQl[:, c, :], start=c == 0, stop=False)

            def lora_out(t):
                mm3(bank[:, fy_bank(t), :], PTh[:, 0, t * P:(t + 1) * P], PTl[:, 0, t * P:(t + 1) * P],
                    WOh[:, 1, :], WOl[:, 1, :], start=False, stop=True).then_inc(sm["fy_mm"], 1)

            need(pe, "f_lo", 7)
            pe.wait_ge(sm["route_in"], 16)
            need(pe, "x_added", NT + NT * HKV)

            def x2_pair(b):
                need(pe, "ln_out", NT + 2 * b + 2)
                for t in (2 * b, 2 * b + 1):
                    x_tile(18 + t, t)
                mean(b).then_inc(sm["mean_mm"], 1)

            x2_pair(0)
            x2_pair(1)
            lora_in(0)
            x2_pair(2)
            x2_pair(3)
            need(pe, "mean_out", 1)
            for c in range(C):
                m = pe.matmul(bank[0:B, 4, 0:E], QT[:, c, :], RWT[:, c, :], start=c == 0, stop=c == C - 1)
            m.then_inc(sm["lg_mm"], 1)
            lora_in(1)
            need(pe, "tr_lo", 26)
            base(0)
            base(1)
            need(pe, "r_out", 1)
            pe.transpose(bank[:, 4, 0:B], R2[:, :], ID[0:B, 0:B]).then_inc(sm["rt_mm"], 1)
            base(2)
            base(3)
            need(pe, "ts_lo", 1)
            for t in range(4):
                lora_out(t)
            need(pe, "ts_lo", 2)
            for t in range(4, NT):
                base(t)
                lora_out(t)

        @block.scalar
        def _(act):
            def copy(o, i):
                return act.activation(o, i, ACT.Copy)

            def tr_hi(n, dst):
                need(act, "tr_mm", n + 1)
                copy(dst, bank[:, PV_BANK + n % 2, :].rearrange("p (c n) -> p c n", n=dst.shape[-1]))\
                    .then_inc(sm["tr_hi"], 1)

            def x_hi(n, t):
                tr_hi(n, XTh[:, :, t * P:(t + 1) * P])

            def gelu(t):
                need(act, "y_mm", t + 1)
                need(act, "x_added", t - 1)
                act.activation(SM[:, t % 2, :], bank[:, y_bank(t), :], ACT.Gelu).then_inc(sm["gelu_done"], 1)

            def wq_hi(g, h):
                act.wait_ge(sm["wq_in"], 16 * (g + 1))
                need(act, "q_mm", 2 * G * (g - 1) + 2 * h + 2)
                copy(WQh[:, :, h * DK:(h + 1) * DK], WQr[:, :, h * DK:(h + 1) * DK]).then_inc(sm["wq_hi"], 1)

            def wo_hi(g):
                act.wait_ge(sm["wo_in"], 16 * (g + 1))
                need(act, "vw_mm", 2 * G * g)
                for h in range(G):
                    copy(WOh[:, h, :], WOr[:, h, :]).then_inc(sm["wo_hi"], 1)

            def wkv_hi(g):
                act.wait_ge(sm["wk_in"], 16 * (g + 1))
                act.wait_ge(sm["wv_in"], 16 * (g + 1))
                need(act, "kv_mm", g)
                copy(KVh[:, :, :, :], KVr[:, :, :, :]).then_inc(sm["wkv_hi"], 1)

            def kv(g):
                need(act, "kv_mm", g + 1)
                need(act, "k_rot", g)
                need(act, "vw_mm", 2 * G * g)
                for lo, hi in ((0, 64), (64, 0)):
                    copy(KSW[lo:lo + 64, :], bank[hi:hi + 64, VW_BANK, 0:B * KS])
                copy(VTh[:, :], bank[:, VW_BANK, B * KS:2 * B * KS]).then_inc(sm["kv_act"], 1)

            def swap(g, h, half):
                i = 2 * G * g + 2 * h + half
                need(act, "q_mm", i + 1)
                need(act, "q_rot", i - 1)
                for lo, hi in ((0, 64), (64, 0)):
                    m = copy(QS[lo:lo + 64, half, :], bank[hi:hi + 64, Q_BANK + half, :])
                m.then_inc(sm["q_swap"], 1)

            def exps(g, h):
                need(act, "s_sub", G * g + h + 1)
                act.activation(SM[:, h % 2, :], SM[:, h % 2, :], ACT.Exp)\
                    .then_inc(sm["s_exp"], 1)

            def pt_hi(g, pair, part):
                need(act, "t_mm", 4 * g + 2 * pair + part + 1)
                if pair == 0 and part == 0:
                    need(act, "pv_mm", NT * g)
                copy(PTh[:, pair, part * HALF:(part + 1) * HALF], bank[:, T_BANK, :]).then_inc(sm["pt_hi"], 1)

            def vw_raw(g, u):
                pair, par, bp = u // 4, u // 2 % 2, u % 2
                need(act, "vw_mm", 2 * G * g + u + 1)
                if par == 0:
                    need(act, "vw_lo", 4 * g + 2 * pair + bp - 1)
                for j in range(2):
                    m = copy(VWr[64 * par:64 * par + 64, bp, j, :], bank[64 * j:64 * j + 64, VW_BANK, :])
                m.then_inc(sm["vw_raw"], 1)

            def group(g, first=False, last=False):
                if first:
                    kv(g)
                    swap(g, 0, 0)
                    for t in range(4, NT):
                        x_hi(10 + t, t)
                    swap(g, 0, 1)
                else:
                    exps(g - 1, 3)
                    swap(g, 0, 0)
                    swap(g, 0, 1)
                if not last:
                    wq_hi(g + 1, 0)
                if not first:
                    pt_hi(g - 1, 1, 0)
                    kv(g)
                    pt_hi(g - 1, 1, 1)
                wo_hi(g)
                if not last:
                    wkv_hi(g + 1)
                swap(g, 1, 0)
                vw_raw(g, 0)
                swap(g, 1, 1)
                vw_raw(g, 1)
                if not last:
                    wq_hi(g + 1, 1)
                exps(g, 0)
                swap(g, 2, 0)
                vw_raw(g, 2)
                swap(g, 2, 1)
                vw_raw(g, 3)
                if not last:
                    wq_hi(g + 1, 2)
                vw_raw(g, 4)
                exps(g, 1)
                swap(g, 3, 0)
                vw_raw(g, 5)
                swap(g, 3, 1)
                vw_raw(g, 6)
                pt_hi(g, 0, 0)
                pt_hi(g, 0, 1)
                exps(g, 2)
                vw_raw(g, 7)
                if not last:
                    wq_hi(g + 1, 3)

            for c in range(C):
                need(act, "w2t_mm", c + 1)
                copy(WQh[:, c, :], bank[:, c, :]).then_inc(sm["w2t_hi"], 1)
            act.wait_ge(sm["w1_in"], 16)
            copy(WOh[:, :, :], WOr[:, :, :]).then_inc(sm["w1_hi"], 1)
            for n in range(2):
                tr_hi(n, CTh[:, 2 * n:2 * n + 2, :])
            act.wait_ge(sm["b2_in"], 16)
            copy(PTh[0:1, 0, 0:D], QS[0:1, 0, :]).then_inc(sm["b2_hi"], 1)
            x_hi(2, 0)
            x_hi(3, 1)
            for s in range(C):
                need(act, "at_masked", s + 1)
                copy(VWh[:, 0, s, :], QA[:, s % 2, :]).then_inc(sm["at_hi"], 1)
                x_hi(4 + s, 2 + s)
            gelu(0)
            x_hi(8, 6)
            wq_hi(0, 0)
            wq_hi(0, 1)
            gelu(1)
            x_hi(9, 7)
            wkv_hi(0)
            gelu(2)
            gelu(3)
            gelu(4)
            x_hi(10, 0)
            x_hi(11, 1)
            gelu(5)
            wq_hi(0, 2)
            gelu(6)
            x_hi(12, 2)
            x_hi(13, 3)
            gelu(7)
            wq_hi(0, 3)

            group(0, first=True)
            with act.Fori(1, LAST) as g:
                group(g)
            group(LAST, last=True)

            exps(LAST, 3)
            f_dst = [WQh[:, 0, :], WQh[:, 1, :], WQh[:, 2, :], WQh[:, 3, :], WOh[:, 0, :], WOh[:, 1, :]]
            for j in range(6):
                need(act, "f_mm", j + 1)
                copy(f_dst[j], bank[:, F_BANKS[j], :]).then_inc(sm["f_hi"], 1)
            pt_hi(LAST, 1, 0)
            pt_hi(LAST, 1, 1)
            for t in range(4):
                x_hi(18 + t, t)
            for t in range(4, NT):
                x_hi(18 + t, t)
            need(act, "lg_step", 3)
            act.activation(LG[:, 2, :], LG[:, 1, :], ACT.Exp).then_inc(sm["lg_exp"], 1)
            need(act, "rt_out", 1)
            for half in range(2):
                need(act, "tt_mm", half + 1)
                for j in range(2):
                    m = act.activation(QS[:, half, j * S:(j + 1) * S], bank[:, (5, 0)[half], j * S:(j + 1) * S],
                                       ACT.Copy, scale=RT[:, 2 * half + j:2 * half + j + 1])
                m.then_inc(sm["ts_out"], 1)
                act.wait_ge(sm["ts_out"], half + 1)
                copy(PTh[:, 0, half * HALF:(half + 1) * HALF], QS[:, half, :]).then_inc(sm["ts_hi"], 1)

        @block.vector
        def _(dve):
            def lo_part(o, i, hi):
                return dve.tensor_tensor(o, i, f32(hi), ALU.subtract)

            def tr_lo(n, hi, lo):
                need(dve, "tr_hi", n + 1)
                lo_part(lo, bank[:, PV_BANK + n % 2, :].rearrange("p (c n) -> p c n", n=lo.shape[-1]), hi)\
                    .then_inc(sm["tr_lo"], 1)

            def x_lo(n, t):
                tr_lo(n, XTh[:, :, t * P:(t + 1) * P], XTl[:, :, t * P:(t + 1) * P])

            def masked(s):
                need(dve, "at_mm", s + 1)
                dve.tensor_tensor(QA[:, s % 2, :], bank[:, (4, 5, 0, 1)[s], :],
                                  VWr[:, s // 2, s % 2, :], ALU.mult).then_inc(sm["at_masked"], 1)
                need(dve, "at_hi", s + 1)
                lo_part(VWl[:, 0, s, :], QA[:, s % 2, :], VWh[:, 0, s, :]).then_inc(sm["at_lo"], 1)

            def stats(k, t):
                n = NT * k + t
                dve.bn_stats(BST[:, t % 2, :], X[:, t, :]).then_inc(sm["ln_stats"], 1)
                need(dve, "ln_stats", n + 1)
                dve.bn_aggr(MV[:, t, :], BST[:, t % 2, :]).then_inc(sm["ln_mean"], 1)

            def guess(k, m):
                i = 3 * (4 * k + m)
                v, r = VE[:, 2 * m:2 * m + 2], RS[:, 2 * m:2 * m + 2]
                need(dve, "ln_mean", NT * k + 2 * m + 2)
                dve.tensor_scalar(v, MV[:, 2 * m:2 * m + 2, 1], LN_EPS, None, ALU.add)
                dve.tensor_scalar(VH[:, 2 * m:2 * m + 2], MV[:, 2 * m:2 * m + 2, 1], LN_EPS, -0.5, ALU.add, ALU.mult)\
                    .then_inc(sm["ln_guess"], 1)
                need(dve, "ln_guess", i + 1)
                dve.tensor_scalar(r.bitcast(I32), v.bitcast(I32), 1, None, ALU.logical_shift_right)\
                    .then_inc(sm["ln_guess"], 1)
                need(dve, "ln_guess", i + 2)
                dve.tensor_scalar(r.bitcast(I32), r.bitcast(I32), -1.0, RSQRT_GUESS, ALU.mult, ALU.add)\
                    .then_inc(sm["ln_guess"], 1)

            def normalize(k, m):
                need(dve, "ln_newton", 4 * NEWTON_STEPS * (4 * k + m + 1))
                for t in (2 * m, 2 * m + 1):
                    dve.tensor_scalar(X[:, t, :], X[:, t, :], MV[:, t, 0:1], RS[:, t:t + 1],
                                      ALU.subtract, ALU.mult).then_inc(sm["ln_out"], 1)

            def residual(t):
                need(dve, "gelu_done", t + 1)
                dve.tensor_tensor(X[:, t, :], X[:, t, :], SM[:, t % 2, :], ALU.add).then_inc(sm["x_added"], 1)
                need(dve, "x_added", t + 1)
                stats(0, t)

            def wkv_lo(g, i):
                need(dve, "wkv_hi", g + 1)
                lo_part(KVl[:, i, :, :], KVr[:, i, :, :], KVh[:, i, :, :]).then_inc(sm["wkv_lo"], 1)

            def wo_lo(g, h):
                need(dve, "wo_hi", G * g + h + 1)
                lo_part(WOl[:, h, :], WOr[:, h, :], WOh[:, h, :]).then_inc(sm["wo_lo"], 1)

            def by_pos(table, copies, n):
                return table[:, 0:n].unsqueeze(1).broadcast_to([P, copies, n])

            def kv_cos(g):
                need(dve, "kv_act", g + 1)
                dve.tensor_tensor(KA[:, :].rearrange("p (b k) -> p b k", b=B),
                                  bank[:, VW_BANK, 0:B * KS].rearrange("p (b k) -> p b k", b=B),
                                  by_pos(COS, B, KS), ALU.mult).then_inc(sm["k_cos"], 1)
                ksw = KSW[:, :].rearrange("p (b k) -> p b k", b=B)
                dve.tensor_tensor(ksw, ksw, by_pos(SIN, B, KS), ALU.mult).then_inc(sm["k_sin"], 1)
                lo_part(VTl[:, :], bank[:, VW_BANK, B * KS:2 * B * KS], VTh[:, :]).then_inc(sm["v_lo"], 1)

            def kv_rot(g):
                need(dve, "k_cos", g + 1)
                need(dve, "k_sin", g + 1)
                need(dve, "s_mm", G * g)
                ka, ksw = (a[:, :].rearrange("p (a b k) -> p a b k", a=2, b=2) for a in (KA, KSW))
                dve.tensor_tensor(KR[:, :, 0:2, :], ka, ksw, ALU.add)
                dve.tensor_tensor(KR[:, :, 2, :], ka[:, :, 0, :], ksw[:, :, 0, :], ALU.add).then_inc(sm["k_rot"], 1)

            def q_cos(g, h, half):
                i = 2 * G * g + 2 * h + half
                need(dve, "q_swap", i + 1)
                dve.tensor_tensor(QA[:, half, :].rearrange("p (b s) -> p b s", b=2),
                                  bank[:, Q_BANK + half, :].rearrange("p (b s) -> p b s", b=2),
                                  by_pos(COS, 2, S), ALU.mult).then_inc(sm["q_cos"], 1)

            def q_rot(g, h, half):
                i = 2 * G * g + 2 * h + half
                need(dve, "q_cos", i + 1)
                need(dve, "q_sin", i + 1)
                if half == 0:
                    need(dve, "s_mm", G * g + h - 1)
                dve.tensor_tensor(QR[:, h % 2, half * HALF:(half + 1) * HALF], QA[:, half, :], QS[:, half, :],
                                  ALU.add).then_inc(sm["q_rot"], 1)

            def soft_max(g, h):
                i = G * g + h
                need(dve, "s_mm", i + 1)
                s = SM[:, h % 2, :].rearrange("p (t k) -> p t k", k=KS)
                need(dve, "p_done", i - 1)
                dve.scalar_tensor_tensor(out=s, in0=bank[:, S_BANK:S_BANK + 2, :].rearrange("p a (t k) -> p (a t) k", k=P)[:, :, 0:KS],
                                         scalar=1.0 / math.sqrt(DK), in1=MSK[:, :, :], op0=ALU.mult, op1=ALU.add)\
                    .then_inc(sm["s_masked"], 1)
                need(dve, "s_masked", i + 1)
                dve.tensor_reduce(MX[:, h % 2, :], s, AX_X, ALU.max).then_inc(sm["s_max"], 1)
                need(dve, "s_max", i + 1)
                dve.tensor_tensor(s, s, MX[:, h % 2, :].unsqueeze(2).broadcast_to([P, NT, KS]), ALU.subtract)\
                    .then_inc(sm["s_sub"], 1)

            def soft_sum(g, h):
                i = G * g + h
                need(dve, "s_exp", i + 1)
                dve.tensor_reduce(SU[:, h % 2, :], SM[:, h % 2, :].rearrange("p (t k) -> p t k", k=KS), AX_X, ALU.add)\
                    .then_inc(sm["s_sum"], 1)
                need(dve, "s_sum", i + 1)
                dve.reciprocal(RI[:, h % 2, :], SU[:, h % 2, :]).then_inc(sm["s_inv"], 1)

            def pt_lo(g, pair, part):
                need(dve, "pt_hi", 4 * g + 2 * pair + part + 1)
                lo_part(PTl[:, pair, part * HALF:(part + 1) * HALF], bank[:, T_BANK, :],
                        PTh[:, pair, part * HALF:(part + 1) * HALF]).then_inc(sm["pt_lo"], 1)

            def vw_hi(g, pair, bp):
                need(dve, "vw_raw", 2 * G * g + 4 * pair + 2 + bp + 1)
                if pair == 0 and bp == 0:
                    need(dve, "pv_mm", NT * g)
                dve.tensor_copy(VWh[:, pair, 2 * bp:2 * bp + 2, :], VWr[:, bp, :, :]).then_inc(sm["vw_hi"], 1)

            def accumulate(g, t):
                need(dve, "pv_mm", NT * g + t + 1)
                dve.tensor_tensor(X[:, t, :], X[:, t, :], bank[:, PV_BANK + t % 2, :], ALU.add)\
                    .then_inc(sm["x_added"], 1)

            def group(g, first=False, last=False):
                if first:
                    normalize(0, 2)
                    kv_cos(g)
                    kv_rot(g)
                    normalize(0, 3)
                    q_cos(g, 0, 0)
                    for t in range(4, NT):
                        x_lo(10 + t, t)
                    q_cos(g, 0, 1)
                    q_rot(g, 0, 0)
                    q_rot(g, 0, 1)
                    for h in range(G):
                        wo_lo(g, h)
                    wkv_lo(g + 1, 0)
                    wkv_lo(g + 1, 1)
                else:
                    soft_max(g - 1, 3)
                    soft_sum(g - 1, 3)
                    q_cos(g, 0, 0)
                    q_cos(g, 0, 1)
                    q_rot(g, 0, 0)
                    q_rot(g, 0, 1)
                    pt_lo(g - 1, 1, 0)
                    pt_lo(g - 1, 1, 1)
                    for t in range(NT):
                        accumulate(g - 1, t)
                        if t == 0:
                            kv_cos(g)
                        elif t == 1:
                            kv_rot(g)
                        elif t < 2 + G:
                            wo_lo(g, t - 2)
                        elif not last:
                            wkv_lo(g + 1, t - 2 - G)
                q_cos(g, 1, 0)
                q_cos(g, 1, 1)
                q_rot(g, 1, 0)
                q_rot(g, 1, 1)
                soft_max(g, 0)
                soft_sum(g, 0)
                q_cos(g, 2, 0)
                q_cos(g, 2, 1)
                q_rot(g, 2, 0)
                vw_hi(g, 0, 0)
                q_rot(g, 2, 1)
                vw_hi(g, 0, 1)
                soft_max(g, 1)
                soft_sum(g, 1)
                q_cos(g, 3, 0)
                q_cos(g, 3, 1)
                q_rot(g, 3, 0)
                pt_lo(g, 0, 0)
                q_rot(g, 3, 1)
                soft_max(g, 2)
                pt_lo(g, 0, 1)
                soft_sum(g, 2)
                vw_hi(g, 1, 0)
                vw_hi(g, 1, 1)

            for c in range(C):
                need(dve, "w2t_hi", c + 1)
                lo_part(WQl[:, c, :], bank[:, c, :], WQh[:, c, :]).then_inc(sm["w2t_lo"], 1)
            need(dve, "w1_hi", 1)
            lo_part(WOl[:, :, :], WOr[:, :, :], WOh[:, :, :]).then_inc(sm["w1_lo"], 1)
            for n in range(2):
                tr_lo(n, CTh[:, 2 * n:2 * n + 2, :], CTl[:, 2 * n:2 * n + 2, :])
            need(dve, "b2_hi", 1)
            lo_part(PTl[0:1, 0, 0:D], QS[0:1, 0, :], PTh[0:1, 0, 0:D]).then_inc(sm["b2_lo"], 1)
            need(dve, "ones_set", 1)
            dve.tensor_copy(PTh[0:1, 1, 0:P], KA[0:1, 0:P]).then_inc(sm["b2_lo"], 1)
            x_lo(2, 0)
            x_lo(3, 1)
            dve.wait_ge(sm["mask_in"], 16)
            for s in range(C):
                masked(s)
                x_lo(4 + s, 2 + s)
            x_lo(8, 6)
            residual(0)
            x_lo(9, 7)
            residual(1)
            guess(0, 0)
            wkv_lo(0, 0)
            wkv_lo(0, 1)
            residual(2)
            residual(3)
            guess(0, 1)
            normalize(0, 0)
            residual(4)
            x_lo(10, 0)
            x_lo(11, 1)
            residual(5)
            guess(0, 2)
            normalize(0, 1)
            residual(6)
            x_lo(12, 2)
            x_lo(13, 3)
            residual(7)
            guess(0, 3)
            dve.wait_ge(sm["rope_in"], 32)
            dve.wait_ge(sm["amask_in"], 16)

            group(0, first=True)
            with dve.Fori(1, LAST) as g:
                group(g)
            group(LAST, last=True)

            soft_max(LAST, 3)
            soft_sum(LAST, 3)
            f_hi = [WQh[:, 0, :], WQh[:, 1, :], WQh[:, 2, :], WQh[:, 3, :], WOh[:, 0, :], WOh[:, 1, :]]
            f_lo = [WQl[:, 0, :], WQl[:, 1, :], WQl[:, 2, :], WQl[:, 3, :], WOl[:, 0, :], WOl[:, 1, :]]
            for j in range(6):
                need(dve, "f_hi", j + 1)
                lo_part(f_lo[j], bank[:, F_BANKS[j], :], f_hi[j]).then_inc(sm["f_lo"], 1)
            need(dve, "f_mm", 7)
            dve.tensor_copy(RWT[:, :, :].rearrange("p c e -> p (c e)"), bank[:, F_BANKS[6], 0:C * E])\
                .then_inc(sm["f_lo"], 1)
            pt_lo(LAST, 1, 0)
            pt_lo(LAST, 1, 1)
            for t in range(NT):
                accumulate(LAST, t)
                need(dve, "x_added", NT + NT * LAST + t + 1)
                stats(1, t)
                if t % 2:
                    guess(1, t // 2)
                if t >= 3 and t % 2:
                    normalize(1, t // 2 - 1)
            normalize(1, 3)
            for t in range(NT):
                x_lo(18 + t, t)
            need(dve, "mean_mm", B)
            dve.tensor_copy(QT[:, :, :].rearrange("p c b -> p (c b)"), bank[:, 1, 0:C * B]).then_inc(sm["mean_out"], 1)
            need(dve, "lg_mm", 1)
            dve.wait_ge(sm["rb_in"], 16)
            dve.tensor_tensor(LG[:, 0, :], bank[0:B, 4, 0:E], RB[:, :], ALU.add).then_inc(sm["lg_step"], 1)
            need(dve, "lg_step", 1)
            dve.tensor_reduce(LS[:, 0:1], LG[:, 0, :], AX_X, ALU.max).then_inc(sm["lg_step"], 1)
            need(dve, "lg_step", 2)
            dve.tensor_scalar(LG[:, 1, :], LG[:, 0, :], LS[:, 0:1], None, ALU.subtract).then_inc(sm["lg_step"], 1)
            need(dve, "lg_exp", 1)
            dve.tensor_reduce(LS[:, 1:2], LG[:, 2, :], AX_X, ALU.add).then_inc(sm["lg_step"], 1)
            need(dve, "lg_step", 4)
            dve.reciprocal(LS[:, 2:3], LS[:, 1:2]).then_inc(sm["lg_step"], 1)
            need(dve, "lg_step", 5)
            dve.tensor_scalar(R2[:, :].rearrange("p (e r) -> p e r", e=E),
                              LG[:, 2, :].unsqueeze(2).broadcast_to([B, E, R]), LS[:, 2:3], LORA_SCALING,
                              ALU.mult, ALU.mult).then_inc(sm["r_out"], 1)
            need(dve, "rt_mm", 1)
            dve.tensor_copy(RT[:, :], bank[:, 4, 0:B]).then_inc(sm["rt_out"], 1)
            for half in range(2):
                need(dve, "ts_hi", half + 1)
                lo_part(PTl[:, 0, half * HALF:(half + 1) * HALF], QS[:, half, :],
                        PTh[:, 0, half * HALF:(half + 1) * HALF]).then_inc(sm["ts_lo"], 1)
            for t in range(NT):
                need(dve, "fy_mm", t + 1)
                need(dve, "bias_in", t + 1)
                dve.tensor_tensor(X[:, t, :], X[:, t, :], bank[:, fy_bank(t), :], ALU.add).then_inc(sm["fy_out"], 1)
                need(dve, "fy_out", t + 1)
                stats(2, t)
                if t % 2:
                    guess(2, t // 2)
                if t >= 3 and t % 2:
                    normalize(2, t // 2 - 1)
            normalize(2, 3)

        @block.gpsimd
        def _(pool):
            def wq_lo(g, h):
                need(pool, "wq_hi", G * g + h + 1)
                w = slice(h * DK, (h + 1) * DK)
                pool.tensor_tensor(WQl[:, :, w], WQr[:, :, w], f32(WQh[:, :, w]), ALU.subtract)\
                    .then_inc(sm["wq_lo"], 1)

            def newton(k, m):
                need(pool, "ln_guess", 3 * (4 * k + m + 1))
                i = 4 * NEWTON_STEPS * (4 * k + m)
                vh, r, w = (a[:, 2 * m:2 * m + 2] for a in (VH, RS, NW))
                for _ in range(NEWTON_STEPS):
                    pool.tensor_tensor(w, r, r, ALU.mult).then_inc(sm["ln_newton"], 1)
                    need(pool, "ln_newton", i + 1)
                    pool.tensor_tensor(w, w, vh, ALU.mult).then_inc(sm["ln_newton"], 1)
                    need(pool, "ln_newton", i + 2)
                    pool.tensor_scalar(w, w, 1.5, None, ALU.add).then_inc(sm["ln_newton"], 1)
                    need(pool, "ln_newton", i + 3)
                    pool.tensor_tensor(r, r, w, ALU.mult).then_inc(sm["ln_newton"], 1)
                    need(pool, "ln_newton", i + 4)
                    i += 4

            def q_sin(g, h, half):
                need(pool, "q_swap", 2 * G * g + 2 * h + half + 1)
                q = QS[:, half, :].rearrange("p (b s) -> p b s", b=2)
                pool.tensor_tensor(q, q, SIN[:, :].unsqueeze(1).broadcast_to([P, 2, S]), ALU.mult)\
                    .then_inc(sm["q_sin"], 1)

            def probs(g, h):
                need(pool, "s_inv", G * g + h + 1)
                if h % 2 == 0:
                    need(pool, "t_mm", 4 * g + h)
                pool.tensor_tensor(PB[:, :, h % 2, :], SM[:, h % 2, :].rearrange("p (t k) -> p t k", k=KS),
                                   RI[:, h % 2, :].unsqueeze(2).broadcast_to([P, NT, KS]), ALU.mult)\
                    .then_inc(sm["p_done"], 1)

            def vw_lo(g, pair, bp):
                need(pool, "vw_hi", 4 * g + 2 * pair + bp + 1)
                pool.tensor_tensor(VWl[:, pair, 2 * bp:2 * bp + 2, :], VWr[:, bp, :, :],
                                   f32(VWh[:, pair, 2 * bp:2 * bp + 2, :]), ALU.subtract).then_inc(sm["vw_lo"], 1)

            def group(g, first=False, last=False):
                q_sin(g, 0, 0)
                if not first:
                    probs(g - 1, 3)
                q_sin(g, 0, 1)
                if not last:
                    wq_lo(g + 1, 0)
                q_sin(g, 1, 0)
                q_sin(g, 1, 1)
                if not last:
                    wq_lo(g + 1, 1)
                probs(g, 0)
                q_sin(g, 2, 0)
                q_sin(g, 2, 1)
                vw_lo(g, 0, 0)
                vw_lo(g, 0, 1)
                probs(g, 1)
                q_sin(g, 3, 0)
                q_sin(g, 3, 1)
                if not last:
                    wq_lo(g + 1, 2)
                vw_lo(g, 1, 0)
                probs(g, 2)
                vw_lo(g, 1, 1)
                if not last:
                    wq_lo(g + 1, 3)

            pool.memset(ID[:, :], 0.0).then_inc(sm["ident"], 1)
            need(pool, "ident", 1)
            pool.affine_select(out=ID[:, :], in_=ID[:, :], compare_op=ALU.not_equal, fill=1.0, base=0,
                               pattern=[[-1, P]], channel_multiplier=1).then_inc(sm["ident"], 1)
            pool.memset(KA[0:1, 0:P], 1.0).then_inc(sm["ones_set"], 1)
            wq_lo(0, 0)
            wq_lo(0, 1)
            pool.wait_ge(sm["rope_in"], 32)
            newton(0, 0)
            newton(0, 1)
            newton(0, 2)
            wq_lo(0, 2)
            wq_lo(0, 3)
            newton(0, 3)

            group(0, first=True)
            with pool.Fori(1, LAST) as g:
                group(g)
            group(LAST, last=True)

            probs(LAST, 3)
            for m in range(4):
                newton(1, m)
            pool.wait_ge(sm["fb_in"], 16)
            for t in range(NT):
                need(pool, "tr_mm", 18 + t + 1)
                need(pool, "mean_mm", t // 2 + 1)
                pool.tensor_tensor(X[:, t, :], X[:, t, :], WOr[:, 3, :], ALU.add).then_inc(sm["bias_in"], 1)
            for m in range(4):
                newton(2, m)


_INS = ['x', 'ctx_4096', 'mask_BxSxS2_ff0', 'L0_attn_w1', 'L0_attn_w2', 'L0_attn_b2', 'L0_attn_sparse_mask', 'L0_xattn_wq', 'L0_xattn_wk',
        'L0_xattn_wv', 'L0_xattn_wo', 'L0_ffn_W', 'L0_ffn_b', 'L0_ffn_A', 'L0_ffn_B', 'L0_ffn_router_W', 'L0_ffn_router_b']


def kernel(**inputs):
    import numpy as _np
    import concourse.bacc as _bacc
    from concourse import mybir as _mybir
    from concourse.bass_utils import run_bass_kernel_spmd as _run

    nc = _bacc.Bacc("TRN2", target_bir_lowering=False, num_devices=1)
    b, s, d = inputs["x"].shape
    arrays, args = {}, []
    given = [(n, inputs[n]) for n in _INS] + [("rope", rope_tables(P, s)), ("route", route_weights(s))]
    for name, a in given:
        a = _np.ascontiguousarray(a)
        arrays[f"in_{name}_dram"] = a
        args.append(nc.dram_tensor(f"in_{name}_dram", a.shape, _mybir.dt.from_np(a.dtype), kind="ExternalInput").ap())
    args.append(nc.dram_tensor("out_0_dram", (b, s, d), F32, kind="ExternalOutput").ap())
    decoder_layer(nc, *args)
    r = _run(nc, [arrays], core_ids=[0])
    return r.results[0]["out_0_dram"]
```

```python
from contextlib import ExitStack
import math

import numpy as np

import concourse.bass as bass
from concourse import mybir

F32 = mybir.dt.float32
F32R = mybir.dt.float32r
I32 = mybir.dt.int32
ACT = mybir.ActivationFunctionType
ALU = mybir.AluOpType
AX_X = mybir.AxisListType.X

P = 128
LN_EPS = 1e-5
RSQRT_GUESS = float(0x5F3759DF)
NEWTON_STEPS = 3
ROUTE_FROM, ROUTE_END = 107, -1
LORA_SCALING = 2.0


def rope_tables(dk, positions):
    inv_freq = (1.0 / np.float32(10000.0) ** (np.arange(0, dk, 2, dtype=np.float32) / np.float32(dk))).astype(np.float32)
    ang = inv_freq[:, None] * np.arange(positions, dtype=np.float32)[None, :]
    cos, sin = np.cos(ang), np.sin(ang)
    return np.stack([np.concatenate([cos, cos]), np.concatenate([-sin, sin])]).astype(np.float32)


def decoder_layer(nc, x, ctx_in, amask, w1, w2, b2, smask, wq, wk, wv, wo, fW, fb, fA, fB, rW, rb, rope, out):
    B, S, D = x.shape
    KS = ctx_in.shape[1]
    HQ, DK = wq.shape[1] // P, P
    HKV = wk.shape[1] // P
    G = HQ // HKV
    E, R = fA.shape[0], fA.shape[1]
    C = D // P
    NT = B * S // P
    TPB = S // P
    HALF = 512
    assert (B, S, D, KS, G, E * R) == (4, 256, 512, 64, 4, 128)

    x_v = x.rearrange("b s d -> (b s) d").rearrange("(t p) d -> p t d", p=P)
    out_v = out.rearrange("b s d -> (b s) d").rearrange("(t p) d -> p t d", p=P)
    amask_v = amask.rearrange("b s k -> (b s) k").rearrange("(t p) k -> p t k", p=P)
    ctx_v = ctx_in.rearrange("b s d -> (b s) d").rearrange("(t p) d -> p t d", p=P)

    def rows(a):
        return a.rearrange("(c p) n -> p c n", p=P)

    with ExitStack() as es:
        def sb(name, shape, dt=F32):
            return es.enter_context(nc.sbuf_tensor(name, shape, dt))

        def sem(name):
            return es.enter_context(nc.semaphore(name))

        X = sb("X", [P, NT, D])
        XTh, XTl = (sb(f"XT{s}", [P, C, B * S], F32R) for s in "hl")
        VWh, VWl = (sb(f"VW{s}", [P, 2, B, D], F32R) for s in "hl")
        WQr = sb("WQr", [P, C, G * DK])
        WQh, WQl = (sb(f"WQ{s}", [P, C, G * DK], F32R) for s in "hl")
        WOr = sb("WOr", [P, G, D])
        WOh, WOl = (sb(f"WO{s}", [P, G, D], F32R) for s in "hl")
        KVr = sb("KVr", [P, 2, C, DK])
        KVh, KVl = (sb(f"KV{s}", [P, 2, C, DK], F32R) for s in "hl")
        CTh, CTl = (sb(f"CT{s}", [P, C, B * KS], F32R) for s in "hl")
        KR = sb("KR", [P, 2, 3, KS])
        KSW = sb("KSW", [P, B * KS])
        KA = sb("KA", [P, B * KS])
        VTh, VTl = (sb(f"VT{s}", [P, B * KS], F32R) for s in "hl")
        QR = sb("QR", [P, 2, B * S])
        QS = sb("QS", [P, 2, HALF])
        QA = sb("QA", [P, 2, HALF])
        PB = sb("PB", [P, 2, NT, 2, KS])
        SM = sb("SM", [P, 2, NT * KS])
        PTh, PTl = (sb(f"PT{s}", [P, 2, B * S], F32R) for s in "hl")
        MSK = sb("MSK", [P, NT, KS])
        COS = sb("COS", [P, S])
        SIN = sb("SIN", [P, S])
        ID = sb("ID", [P, P])
        MX = sb("MX", [P, 2, NT])
        SU = sb("SU", [P, 2, NT])
        RI = sb("RI", [P, 2, NT])
        BST = sb("BST", [P, 2, 6])
        MV = sb("MV", [P, NT, 2])
        VE = sb("VE", [P, NT])
        RS = sb("RS", [P, NT])
        NW = sb("NW", [P, NT])
        NM = sb("NM", [P, NT])
        VH = sb("VH", [P, NT])
        TS = sb("TS", [P, NT, C])
        QT = sb("QT", [P, C, B])
        RWT = sb("RWT", [P, C, E])
        RB = sb("RB", [B, E])
        LG = sb("LG", [B, 4, E])
        LS = sb("LS", [B, 4])
        R2 = sb("R2", [B, E * R])
        RT = sb("RT", [P, B])

        bank = es.enter_context(nc.psum_tensor("bank", [P, 8, 512], F32))
        Q_BANK, S_BANK, T_BANK, VW_BANK, PV_BANK = 0, 2, 4, 5, 6

        names = """mask_in ctx_in_ b2_in rope_in wq_in wo_in wk_in wv_in fw_in fa_in fbm_in rw_in rb_in
        fb_in amask_in stored ident ones_set w2t_mm w2t_hi w2t_lo w1_hi w1_lo_even w1_lo_odd b2_hi b2_lo tr_mm tr_hi tr_lo
        at_mm at_masked at_hi at_lo y_mm gelu_done x_added ln_stats ln_mean ln_guess ln_newton ln_out ln_shift last_shift out_done out_even
        wq_hi wq_lo wo_hi wo_lo wkv_hi wkv_lo kv_mm kv_act k_cos k_sin k_rot v_lo
        q_mm q_swap q_cos q_sin q_rot s_mm s_masked s_max s_sub s_exp s_sum s_inv p_done
        t_mm pt_hi pt_lo vw_mm vw_hi vw_lo pv_mm
        f_mm f_hi f_lo tile_sum mean_out lg_mm lg_step lg_exp r_out rt_mm rt_out tt_mm ts_out ts_hi ts_lo
        fy_mm fy_out bias_in""".split()
        sm = {n: sem(n) for n in names}
        x_in = [sem(f"x_in{i}") for i in range(5)]
        w1_in, w2_in = ([sem(f"{w}_in{c}") for c in range(C)] for w in ("w1", "w2"))

        def counted(value):
            return not isinstance(value, int) or value > 0

        SMASK = PB[:, :, :, :, :].rearrange("p i t a k -> p (i t a k)").rearrange("p (c n) -> p c n", n=D)
        block = es.enter_context(nc.Block())
        f32 = lambda ap: ap.bitcast(F32)

        def vw_bank(u):
            return (T_BANK, VW_BANK)[u % 2]

        def t_bank(part):
            return (T_BANK, PV_BANK + 1)[part]

        def tr_bank(n):
            return (S_BANK if n in (16, 17, 18, 19) else PV_BANK) + n % 2

        def y_bank(t):
            return 2 + t % 2

        def fy_bank(t):
            return (0, 1, 2, 3, 6, 7, 0, 1)[t]

        F_BANKS = (6, 0, 1, 5, 0, 1, 5)
        LORA_BANK, LG_BANK, RT_BANK = 4, 7, 7
        LAST = HKV - 1

        @block.sync
        def _(sp):
            def load(dst, src, name):
                sp.dma_start(dst, src).then_inc(sm[name], 16)

            for c in range(C):
                sp.dma_start(WQr[:, c, :], rows(w2)[:, c, :]).then_inc(w2_in[c], 16)
            for c in range(C):
                sp.dma_start(WOr[:, c, :], rows(w1)[:, c, :]).then_inc(w1_in[c], 16)
            for i in range(2):
                sp.dma_start(X[:, i, :], x_v[:, i, :]).then_inc(x_in[i], 16)
            load(SMASK, rows(smask), "mask_in")
            sp.dma_start(X[:, 2:4, :], x_v[:, 2:4, :]).then_inc(x_in[2], 16)
            load(QR[:, :, 0:D], ctx_v, "ctx_in_")
            load(QS[0:1, 0, :], b2.rearrange("(a n) -> a n", a=1), "b2_in")
            for i in (2, 3):
                sp.dma_start(X[:, 2 * i:2 * i + 2, :], x_v[:, 2 * i:2 * i + 2, :]).then_inc(x_in[i + 1], 16)
            load(KVr[:, 0, :, :], rows(wk)[:, :, 0:DK], "wk_in")
            load(KVr[:, 1, :, :], rows(wv)[:, :, 0:DK], "wv_in")
            load(COS[:, :], rope[0, :, :], "rope_in")
            load(SIN[:, :], rope[1, :, :], "rope_in")
            load(MSK[:, :, :], amask_v, "amask_in")
            load(RB[:, :], rb.rearrange("(a n) -> a n", a=1).broadcast_to([B, E]), "rb_in")
            sp.wait_ge(sm["w2t_mm"], C)
            load(WQr[:, :, :], rows(wq)[:, :, 0:G * DK], "wq_in")
            sp.wait_ge(sm["w1_lo_even"], 2)
            sp.wait_ge(sm["w1_lo_odd"], 2)
            load(WOr[:, :, :], rows(wo[0:G * DK, :]), "wo_in")
            with sp.Fori(1, HKV) as g:
                kv_at, q_at = sp.snap(g * DK), sp.snap(g * G * DK)
                sp.wait_ge(sm["wkv_lo"], 2 * g)
                load(KVr[:, 0, :, :], rows(wk)[:, :, bass.ds(kv_at, DK)], "wk_in")
                load(KVr[:, 1, :, :], rows(wv)[:, :, bass.ds(kv_at, DK)], "wv_in")
                sp.wait_ge(sm["wq_lo"], g * G)
                load(WQr[:, :, :], rows(wq)[:, :, bass.ds(q_at, G * DK)], "wq_in")
                sp.wait_ge(sm["wo_lo"], g * G)
                load(WOr[:, :, :], rows(wo[bass.ds(q_at, G * DK), :]), "wo_in")
            sp.wait_ge(sm["wq_lo"], HKV * G)
            load(WQr[:, :, :], rows(fW), "fw_in")
            sp.wait_ge(sm["wo_lo"], HKV * G)
            load(WOr[:, 0, :], fA.rearrange("e r d -> (e r) d"), "fa_in")
            for oc in range(C):
                load(WOr[:, 1, oc * P:(oc + 1) * P].rearrange("p (e r) -> p e r", e=E),
                     fB[:, oc * P:(oc + 1) * P, :].rearrange("e p r -> p e r"), "fbm_in")
            load(WOr[0:E, 2, :], rW, "rw_in")
            load(WOr[:, 3, :], fb.rearrange("(a n) -> a n", a=1).broadcast_to([P, D]), "fb_in")
            for t in range(NT):
                if t == 6:
                    sp.wait_ge(sm["out_even"], 1)
                else:
                    sp.wait_ge(sm["out_done"], min(t + 1, 7))
                load(out_v[:, t, :], X[:, t, :], "stored")
            sp.wait_ge(sm["stored"], 16 * NT)

        @block.tensor
        def _(pe):
            def mm3(o, lh, ll, rh, rl, start=True, stop=True):
                pe.matmul(o, lh, rh, start=start, stop=False)
                pe.matmul(o, lh, rl, start=False, stop=False)
                return pe.matmul(o, ll, rh, start=False, stop=stop)

            def transpose_tile(n, tiles):
                if n not in (16, 17):
                    if counted(n - 1):
                        pe.wait_ge(sm["tr_lo"], n - 1)
                for out_at, src in tiles:
                    m = pe.transpose(bank[:, tr_bank(n), out_at:out_at + P], src, ID[:, :])
                m.then_inc(sm["tr_mm"], 1)

            def x_tile(n, t):
                transpose_tile(n, [(c * P, X[:, t, c * P:(c + 1) * P]) for c in range(C)])

            def attn_weights(s):
                for c in range(C):
                    if s == 0:
                        pe.wait_ge(sm[("w1_lo_even", "w1_lo_odd")[c % 2]], c // 2 + 1)
                    m = mm3(bank[:, (4, 5, 0, 1)[s], :], WOh[:, c, s * P:(s + 1) * P], WOl[:, c, s * P:(s + 1) * P],
                            WQh[:, c, :], WQl[:, c, :], start=c == 0, stop=c == C - 1)
                m.then_inc(sm["at_mm"], 1)

            def dense(t):
                pe.wait_ge(sm["tr_lo"], t + 1 + (2 if t > 3 else 0))
                if counted(t - 1):
                    pe.wait_ge(sm["gelu_done"], t - 1)
                o = bank[:, y_bank(t), :]
                pe.matmul(o, PTh[0:1, 1, 0:P], PTh[0:1, 0, 0:D], start=True, stop=False)
                pe.matmul(o, PTh[0:1, 1, 0:P], PTl[0:1, 0, 0:D], start=False, stop=False)
                for s in range(C):
                    if t == 0:
                        pe.wait_ge(sm["at_lo"], s + 1)
                    m = mm3(o, XTh[:, s, t * P:(t + 1) * P], XTl[:, s, t * P:(t + 1) * P],
                            VWh[:, 0, s, :], VWl[:, 0, s, :], start=False, stop=s == C - 1)
                m.then_inc(sm["y_mm"], 1)

            def keys(g):
                pe.wait_ge(sm["wkv_lo"], 2 * g + 1)
                if counted(2 * G * g):
                    pe.wait_ge(sm["vw_lo"], 2 * G * g)
                for c in range(C):
                    mm3(bank[:, VW_BANK, 0:B * KS], KVh[:, 0, c, :], KVl[:, 0, c, :], CTh[:, c, :], CTl[:, c, :],
                        start=c == 0, stop=c == C - 1)

            def values(g):
                pe.wait_ge(sm["wkv_lo"], 2 * g + 2)
                for c in range(C):
                    m = mm3(bank[:, VW_BANK, B * KS:2 * B * KS], KVh[:, 1, c, :], KVl[:, 1, c, :],
                            CTh[:, c, :], CTl[:, c, :], start=c == 0, stop=c == C - 1)
                m.then_inc(sm["kv_mm"], 1)

            def query(g, h, half):
                pe.wait_ge(sm["wq_lo"], G * g + h + 1)
                if counted(2 * G * g + 2 * h + half - 1):
                    pe.wait_ge(sm["q_cos"], 2 * G * g + 2 * h + half - 1)
                for c in range(C):
                    m = mm3(bank[:, Q_BANK + half, :], WQh[:, c, h * DK:(h + 1) * DK], WQl[:, c, h * DK:(h + 1) * DK],
                            XTh[:, c, half * HALF:(half + 1) * HALF], XTl[:, c, half * HALF:(half + 1) * HALF],
                            start=c == 0, stop=c == C - 1)
                m.then_inc(sm["q_mm"], 1)

            def scores(g, h):
                pe.wait_ge(sm["q_rot"], 2 * G * g + 2 * h + 2)
                pe.wait_ge(sm["k_rot"], g + 1)
                if counted(G * g + h):
                    pe.wait_ge(sm["s_masked"], G * g + h)
                for t in range(NT):
                    b = t // TPB
                    m = pe.matmul(bank[:, S_BANK + t // 4, t % 4 * P:(t % 4 + 1) * P], QR[:, h % 2, t * P:(t + 1) * P],
                                  KR[:, b // 2, b % 2:b % 2 + 2, :].rearrange("p b k -> p (b k)"), start=True, stop=True)
                m.then_inc(sm["s_mm"], 1)

            def probs_transpose(g, pair, part):
                pe.wait_ge(sm["p_done"], G * g + 2 * pair + 2)
                if counted(4 * g + 2 * pair + part - 1):
                    pe.wait_ge(sm["pt_lo"], 4 * g + 2 * pair + part - 1)
                if pair == 0 and part == 0:
                    pe.wait_ge(sm["vw_lo"], 2 * G * g + 7)
                elif pair == 0:
                    pe.wait_ge(sm["x_added"], NT + NT * g)
                for j in range(4):
                    m = pe.transpose(bank[:, t_bank(part), j * P:(j + 1) * P],
                                     PB[:, pair, 4 * part + j, :, :].rearrange("p a k -> p (a k)"), ID[:, :])
                m.then_inc(sm["t_mm"], 1)

            def value_out(g, u):
                pair, par, bp = u // 4, u // 2 % 2, u % 2
                h = 2 * pair + par
                pe.wait_ge(sm["wo_lo"], G * g + h + 1)
                pe.wait_ge(sm["v_lo"], g + 1)
                if counted(2 * G * g + u - 1):
                    pe.wait_ge(sm["vw_lo"], 2 * G * g + u - 1)
                mm3(bank[:, vw_bank(u), :], VTh[:, bp * P:(bp + 1) * P], VTl[:, bp * P:(bp + 1) * P],
                    WOh[:, h, :], WOl[:, h, :]).then_inc(sm["vw_mm"], 1)

            def attend(g, t):
                pe.wait_ge(sm["pt_lo"], 4 * g + (3 if t == 0 else 4))
                pe.wait_ge(sm["vw_lo"], 2 * G * (g + 1))
                pe.wait_ge(sm["x_added"], NT + NT * g + t - 1)
                for pair in range(2):
                    m = mm3(bank[:, PV_BANK + t % 2, :], PTh[:, pair, t * P:(t + 1) * P], PTl[:, pair, t * P:(t + 1) * P],
                            VWh[:, pair, t // TPB, :], VWl[:, pair, t // TPB, :], start=pair == 0, stop=pair == 1)
                m.then_inc(sm["pv_mm"], 1)

            def group(g, first=False):
                if first:
                    for t in range(4, NT):
                        pe.wait_ge(sm["ln_out"], t + 1)
                        pe.wait_ge(sm["gelu_done"], t + 1)
                        x_tile(10 + t, t)
                        if t == 4:
                            keys(g)
                            values(g)
                            pe.wait_ge(sm["tr_lo"], 14)
                            query(g, 0, 0)
                    pe.wait_ge(sm["tr_lo"], 18)
                    query(g, 0, 1)
                if not first:
                    query(g, 0, 0)
                    query(g, 0, 1)
                    keys(g)
                    scores(g - 1, 3)
                    values(g)
                query(g, 1, 0)
                query(g, 1, 1)
                if not first:
                    probs_transpose(g - 1, 1, 0)
                    probs_transpose(g - 1, 1, 1)
                query(g, 2, 0)
                if not first:
                    attend(g - 1, 0)
                scores(g, 0)
                if not first:
                    for t in range(1, 4):
                        attend(g - 1, t)
                value_out(g, 0)
                if not first:
                    for t in range(4, 8):
                        attend(g - 1, t)
                value_out(g, 1)
                query(g, 2, 1)
                value_out(g, 2)
                scores(g, 1)
                value_out(g, 3)
                query(g, 3, 0)
                value_out(g, 4)
                value_out(g, 5)
                query(g, 3, 1)
                value_out(g, 6)
                scores(g, 2)
                value_out(g, 7)
                probs_transpose(g, 0, 0)
                probs_transpose(g, 0, 1)

            pe.wait_ge(sm["ident"], 2)
            for t in range(C):
                pe.wait_ge(w2_in[t], 16)
                for c in range(C):
                    m = pe.transpose(bank[:, t, c * P:(c + 1) * P], WQr[:, t, c * P:(c + 1) * P], ID[:, :])
                m.then_inc(sm["w2t_mm"], 1)
            pe.wait_ge(sm["w2t_lo"], C)
            attn_weights(0)
            for t in range(2):
                pe.wait_ge(x_in[t], 16)
                x_tile(t, t)
            attn_weights(1)
            pe.wait_ge(x_in[2], 16)
            x_tile(2, 2)
            attn_weights(2)
            x_tile(3, 3)
            attn_weights(3)
            pe.wait_ge(sm["ctx_in_"], 16)
            for n in range(2):
                transpose_tile(4 + n, [(256 * j + r * P, QR[:, r, (2 * n + j) * P:(2 * n + j + 1) * P])
                                       for j in range(2) for r in range(2)])
            pe.wait_ge(sm["b2_lo"], 2)
            dense(0)
            pe.wait_ge(x_in[3], 16)
            x_tile(6, 4)
            dense(1)
            x_tile(7, 5)
            dense(2)
            pe.wait_ge(x_in[4], 16)
            x_tile(8, 6)
            dense(3)
            x_tile(9, 7)
            dense(4)
            pe.wait_ge(sm["ln_out"], 2)
            x_tile(10, 0)
            dense(5)
            x_tile(11, 1)
            dense(6)
            pe.wait_ge(sm["ln_out"], 4)
            x_tile(12, 2)
            dense(7)
            x_tile(13, 3)

            group(0, first=True)
            with pe.Fori(1, HKV) as g:
                group(g)

            def weight_transpose(j):
                if counted(j - 2):
                    pe.wait_ge(sm["f_lo"], j - 2)
                for name, first, value in (("fw_in", 0, 16), ("fa_in", 4, 16), ("fbm_in", 5, 16 * C), ("rw_in", 6, 16)):
                    if j == first:
                        pe.wait_ge(sm[name], value)
                o = bank[:, F_BANKS[j], :]
                for t in range(C):
                    src = WQr[:, t, j * P:(j + 1) * P] if j < 4 else WOr[:, j - 4, t * P:(t + 1) * P]
                    if j == 6:
                        m = pe.transpose(o[:, t * E:(t + 1) * E], src[0:E, :], ID[0:E, 0:E])
                    else:
                        m = pe.transpose(o[:, t * P:(t + 1) * P], src, ID[:, :])
                m.then_inc(sm["f_mm"], 1)

            pe.wait_ge(sm["x_added"], NT + NT * LAST)
            weight_transpose(0)
            pe.wait_ge(sm["q_cos"], 2 * G * HKV)
            weight_transpose(1)
            weight_transpose(2)
            scores(LAST, 3)
            pe.wait_ge(sm["vw_lo"], 2 * G * HKV)
            weight_transpose(3)
            weight_transpose(4)
            probs_transpose(LAST, 1, 0)
            probs_transpose(LAST, 1, 1)
            weight_transpose(5)
            weight_transpose(6)
            pe.wait_ge(sm["f_lo"], 1)
            for t in range(NT - 1):
                attend(LAST, t)

            def x2_tiles(m):
                for t in (2 * m, 2 * m + 1):
                    pe.wait_ge(sm["ln_out"], NT + t + 1)
                    x_tile(18 + t, t)

            def lora_in(half):
                pe.wait_ge(sm["tr_lo"], 18 + 4 * (half + 1))
                for c in range(C):
                    m = mm3(bank[:, LORA_BANK + half, :], WOh[:, 0, c * P:(c + 1) * P], WOl[:, 0, c * P:(c + 1) * P],
                            XTh[:, c, half * HALF:(half + 1) * HALF], XTl[:, c, half * HALF:(half + 1) * HALF],
                            start=c == 0, stop=c == C - 1)
                m.then_inc(sm["tt_mm"], 1)

            def base(t):
                if t == 5:
                    pe.wait_ge(sm["rt_out"], 1)
                if t >= 6:
                    pe.wait_ge(sm["fy_out"], t - 5)
                pe.wait_ge(sm["tr_lo"], 18 + t + 1)
                for c in range(C):
                    mm3(bank[:, fy_bank(t), :], XTh[:, c, t * P:(t + 1) * P], XTl[:, c, t * P:(t + 1) * P],
                        WQh[:, c, :], WQl[:, c, :], start=c == 0, stop=False)

            def lora_out(t):
                pe.wait_ge(sm["ts_lo"], t // 4 + 1)
                mm3(bank[:, fy_bank(t), :], PTh[:, 0, t * P:(t + 1) * P], PTl[:, 0, t * P:(t + 1) * P],
                    WOh[:, 1, :], WOl[:, 1, :], start=False, stop=True).then_inc(sm["fy_mm"], 1)

            pe.wait_ge(sm["s_masked"], G * HKV)
            x2_tiles(0)
            attend(LAST, NT - 1)
            pe.wait_ge(sm["f_lo"], 7)
            base(0)
            pe.wait_ge(sm["x_added"], NT + NT * HKV)
            x2_tiles(1)
            base(1)
            lora_in(0)
            x2_tiles(2)
            base(2)
            x2_tiles(3)
            base(3)
            lora_in(1)
            pe.wait_ge(sm["mean_out"], 1)
            for c in range(C):
                m = pe.matmul(bank[0:B, LG_BANK, 0:E], QT[:, c, :], RWT[:, c, :], start=c == 0, stop=c == C - 1)
            m.then_inc(sm["lg_mm"], 1)
            base(4)
            pe.wait_ge(sm["r_out"], 1)
            pe.transpose(bank[:, RT_BANK, 0:B], R2[:, :], ID[0:B, 0:B]).then_inc(sm["rt_mm"], 1)
            base(5)
            for t in range(6):
                lora_out(t)
            for t in range(6, NT):
                base(t)
                lora_out(t)

        @block.scalar
        def _(act):
            def copy(o, i):
                return act.activation(o, i, ACT.Copy)

            def tr_hi(n, dst):
                act.wait_ge(sm["tr_mm"], n + 1)
                copy(dst, bank[:, tr_bank(n), :].rearrange("p (c n) -> p c n", n=dst.shape[-1]))\
                    .then_inc(sm["tr_hi"], 1)

            def x_hi(n, t):
                tr_hi(n, XTh[:, :, t * P:(t + 1) * P])

            def gelu(t):
                act.wait_ge(sm["y_mm"], t + 1)
                if counted(t - 1):
                    act.wait_ge(sm["x_added"], t - 1)
                act.activation(SM[:, t % 2, :], bank[:, y_bank(t), :], ACT.Gelu).then_inc(sm["gelu_done"], 1)

            def wq_hi(g, h):
                act.wait_ge(sm["wq_in"], 16 * (g + 1))
                if counted(2 * G * (g - 1) + 2 * h + 2):
                    act.wait_ge(sm["q_mm"], 2 * G * (g - 1) + 2 * h + 2)
                copy(WQh[:, :, h * DK:(h + 1) * DK], WQr[:, :, h * DK:(h + 1) * DK]).then_inc(sm["wq_hi"], 1)

            def wo_hi(g):
                act.wait_ge(sm["wo_in"], 16 * (g + 1))
                if counted(2 * G * g):
                    act.wait_ge(sm["vw_mm"], 2 * G * g)
                if isinstance(g, int) and g == 0:
                    act.wait_ge(sm["at_mm"], C)
                for h in range(G):
                    copy(WOh[:, h, :], WOr[:, h, :]).then_inc(sm["wo_hi"], 1)

            def wkv_hi(g):
                act.wait_ge(sm["wk_in"], 16 * (g + 1))
                act.wait_ge(sm["wv_in"], 16 * (g + 1))
                if counted(g):
                    act.wait_ge(sm["kv_mm"], g)
                copy(KVh[:, :, :, :], KVr[:, :, :, :]).then_inc(sm["wkv_hi"], 1)

            def kv(g):
                act.wait_ge(sm["kv_mm"], g + 1)
                if counted(g):
                    act.wait_ge(sm["k_rot"], g)
                if counted(2 * G * g):
                    act.wait_ge(sm["vw_mm"], 2 * G * g)
                for lo, hi in ((0, 64), (64, 0)):
                    copy(KSW[lo:lo + 64, :], bank[hi:hi + 64, VW_BANK, 0:B * KS])
                copy(VTh[:, :], bank[:, VW_BANK, B * KS:2 * B * KS]).then_inc(sm["kv_act"], 1)

            def swap(g, h, half):
                i = 2 * G * g + 2 * h + half
                act.wait_ge(sm["q_mm"], i + 1)
                if counted(i - 1):
                    act.wait_ge(sm["q_rot"], i - 1)
                for lo, hi in ((0, 64), (64, 0)):
                    m = copy(QS[lo:lo + 64, half, :], bank[hi:hi + 64, Q_BANK + half, :])
                m.then_inc(sm["q_swap"], 1)

            def exps(g, h):
                act.wait_ge(sm["s_sub"], G * g + h + 1)
                act.activation(SM[:, h % 2, :], SM[:, h % 2, :], ACT.Exp)\
                    .then_inc(sm["s_exp"], 1)

            def pt_hi(g, pair, part):
                act.wait_ge(sm["t_mm"], 4 * g + 2 * pair + part + 1)
                if pair == 0 and part == 0:
                    if counted(NT * g):
                        act.wait_ge(sm["pv_mm"], NT * g)
                copy(PTh[:, pair, part * HALF:(part + 1) * HALF], bank[:, t_bank(part), :]).then_inc(sm["pt_hi"], 1)

            def vw_hi(g, u):
                pair, par, bp = u // 4, u // 2 % 2, u % 2
                act.wait_ge(sm["vw_mm"], 2 * G * g + u + 1)
                if u == 0:
                    if counted(NT * g):
                        act.wait_ge(sm["pv_mm"], NT * g)
                for j in range(2):
                    m = copy(VWh[64 * par:64 * par + 64, pair, 2 * bp + j, :], bank[64 * j:64 * j + 64, vw_bank(u), :])
                m.then_inc(sm["vw_hi"], 1)

            def group(g, first=False, last=False):
                if first:
                    x_hi(14, 4)
                    kv(g)
                    for t in range(5, NT):
                        x_hi(10 + t, t)
                    swap(g, 0, 0)
                    swap(g, 0, 1)
                if not first:
                    swap(g, 0, 0)
                    swap(g, 0, 1)
                if not first:
                    wo_hi(g)
                if not first:
                    kv(g)
                    exps(g - 1, 3)
                if not last:
                    wq_hi(g + 1, 0)
                swap(g, 1, 0)
                swap(g, 1, 1)
                if not first:
                    pt_hi(g - 1, 1, 0)
                if not last:
                    wkv_hi(g + 1)
                if not first:
                    pt_hi(g - 1, 1, 1)
                swap(g, 2, 0)
                exps(g, 0)
                vw_hi(g, 0)
                vw_hi(g, 1)
                if not last:
                    wq_hi(g + 1, 1)
                swap(g, 2, 1)
                for i in range(2, 5):
                    vw_hi(g, i)
                if not last:
                    wq_hi(g + 1, 2)
                exps(g, 1)
                vw_hi(g, 5)
                vw_hi(g, 6)
                swap(g, 3, 0)
                swap(g, 3, 1)
                vw_hi(g, 7)
                pt_hi(g, 0, 0)
                if not last:
                    wq_hi(g + 1, 3)
                exps(g, 2)
                pt_hi(g, 0, 1)

            for t in range(C):
                act.wait_ge(sm["w2t_mm"], t + 1)
                copy(WQh[:, :, t * P:(t + 1) * P], bank[:, t, :].rearrange("p (c n) -> p c n", n=P)).then_inc(sm["w2t_hi"], 1)
            for c in range(C):
                act.wait_ge(w1_in[c], 16)
                copy(WOh[:, c, :], WOr[:, c, :]).then_inc(sm["w1_hi"], 1)
            x_hi(0, 0)
            x_hi(1, 1)
            act.wait_ge(sm["b2_in"], 16)
            copy(PTh[0:1, 0, 0:D], QS[0:1, 0, :]).then_inc(sm["b2_hi"], 1)

            def at_hi(s):
                act.wait_ge(sm["at_masked"], s + 1)
                copy(VWh[:, 0, s, :], QA[:, s % 2, :]).then_inc(sm["at_hi"], 1)

            at_hi(0)
            at_hi(1)
            x_hi(2, 2)
            at_hi(2)
            x_hi(3, 3)
            tr_hi(4, CTh[:, 0:2, :])
            at_hi(3)
            tr_hi(5, CTh[:, 2:4, :])
            wq_hi(0, 0)
            wkv_hi(0)
            gelu(0)
            x_hi(6, 4)
            gelu(1)
            x_hi(7, 5)
            wq_hi(0, 1)
            wo_hi(0)
            gelu(2)
            x_hi(8, 6)
            gelu(3)
            x_hi(9, 7)
            wq_hi(0, 2)
            gelu(4)
            x_hi(10, 0)
            wq_hi(0, 3)
            gelu(5)
            x_hi(11, 1)
            gelu(6)
            x_hi(12, 2)
            gelu(7)
            x_hi(13, 3)

            group(0, first=True)
            with act.Fori(1, LAST) as g:
                group(g)
            group(LAST, last=True)

            f_dst = [WQh[:, 0, :], WQh[:, 1, :], WQh[:, 2, :], WQh[:, 3, :], WOh[:, 0, :], WOh[:, 1, :]]

            def f_hi(j):
                act.wait_ge(sm["f_mm"], j + 1)
                copy(f_dst[j], bank[:, F_BANKS[j], :]).then_inc(sm["f_hi"], 1)

            for j in range(3):
                f_hi(j)
            exps(LAST, 3)
            f_hi(3)
            f_hi(4)
            pt_hi(LAST, 1, 0)
            pt_hi(LAST, 1, 1)
            f_hi(5)
            for t in range(NT):
                x_hi(18 + t, t)
            act.wait_ge(sm["lg_step"], 3)
            act.activation(LG[:, 2, :], LG[:, 1, :], ACT.Exp).then_inc(sm["lg_exp"], 1)
            act.wait_ge(sm["rt_out"], 1)
            for half in range(2):
                act.wait_ge(sm["tt_mm"], half + 1)
                for j in range(2):
                    m = act.activation(QS[:, half, j * S:(j + 1) * S], bank[:, LORA_BANK + half, j * S:(j + 1) * S],
                                       ACT.Copy, scale=RT[:, 2 * half + j:2 * half + j + 1])
                m.then_inc(sm["ts_out"], 1)
                act.wait_ge(sm["ts_out"], half + 1)
                copy(PTh[:, 0, half * HALF:(half + 1) * HALF], QS[:, half, :]).then_inc(sm["ts_hi"], 1)
            for t in (0, 1, 2, 3, 4, 5, 7):
                if t < 6:
                    act.wait_ge(sm["ln_shift"], 2 * (t // 2 + 1))
                else:
                    act.wait_ge(sm["last_shift"], 2)
                act.activation(X[:, t, :], X[:, t, :], ACT.Identity, bias=NM[:, t:t + 1], scale=RS[:, t:t + 1])\
                    .then_inc(sm["out_done"], 1)

        @block.vector
        def _(dve):
            def lo_part(o, i, hi):
                return dve.tensor_tensor(o, i, f32(hi), ALU.subtract)

            def tr_lo(n, hi, lo):
                dve.wait_ge(sm["tr_hi"], n + 1)
                lo_part(lo, bank[:, tr_bank(n), :].rearrange("p (c n) -> p c n", n=lo.shape[-1]), hi)\
                    .then_inc(sm["tr_lo"], 1)

            def x_lo(n, t):
                tr_lo(n, XTh[:, :, t * P:(t + 1) * P], XTl[:, :, t * P:(t + 1) * P])

            def masked(s):
                dve.wait_ge(sm["at_mm"], s + 1)
                dve.tensor_tensor(QA[:, s % 2, :], bank[:, (4, 5, 0, 1)[s], :],
                                  SMASK[:, s, :], ALU.mult).then_inc(sm["at_masked"], 1)
                dve.wait_ge(sm["at_hi"], s + 1)
                lo_part(VWl[:, 0, s, :], QA[:, s % 2, :], VWh[:, 0, s, :]).then_inc(sm["at_lo"], 1)

            def stats(k, t):
                n = NT * k + t
                dve.bn_stats(BST[:, t % 2, :], X[:, t, :]).then_inc(sm["ln_stats"], 1)
                dve.wait_ge(sm["ln_stats"], n + 1)
                dve.bn_aggr(MV[:, t, :], BST[:, t % 2, :]).then_inc(sm["ln_mean"], 1)

            def guess(k, m):
                i = 3 * (4 * k + m)
                v, r = VE[:, 2 * m:2 * m + 2], RS[:, 2 * m:2 * m + 2]
                dve.wait_ge(sm["ln_mean"], NT * k + 2 * m + 2)
                dve.tensor_scalar(v, MV[:, 2 * m:2 * m + 2, 1], LN_EPS, None, ALU.add)
                dve.tensor_scalar(VH[:, 2 * m:2 * m + 2], MV[:, 2 * m:2 * m + 2, 1], LN_EPS, -0.5, ALU.add, ALU.mult)\
                    .then_inc(sm["ln_guess"], 1)
                dve.wait_ge(sm["ln_guess"], i + 1)
                dve.tensor_scalar(r.bitcast(I32), v.bitcast(I32), 1, None, ALU.logical_shift_right)\
                    .then_inc(sm["ln_guess"], 1)
                dve.wait_ge(sm["ln_guess"], i + 2)
                dve.tensor_scalar(r.bitcast(I32), r.bitcast(I32), -1.0, RSQRT_GUESS, ALU.mult, ALU.add)\
                    .then_inc(sm["ln_guess"], 1)

            def newton(k, m):
                dve.wait_ge(sm["ln_guess"], 3 * (4 * k + m + 1))
                i = 4 * NEWTON_STEPS * (4 * k + m)
                dve.wait_ge(sm["ln_newton"], i)
                vh, r, w = ([a[:, t:t + 1] for t in (2 * m, 2 * m + 1)] for a in (VH, RS, NW))
                for _ in range(NEWTON_STEPS):
                    for j in range(2):
                        dve.wait_ge(sm["ln_newton"], i - 1 + j)
                        dve.tensor_scalar(w[j], r[j], r[j], vh[j], ALU.mult, ALU.mult).then_inc(sm["ln_newton"], 1)
                    for j in range(2):
                        dve.wait_ge(sm["ln_newton"], i + 1 + j)
                        dve.tensor_scalar(r[j], w[j], 1.5, r[j], ALU.add, ALU.mult).then_inc(sm["ln_newton"], 1)
                    i += 4

            def normalize(k, m):
                dve.wait_ge(sm["ln_newton"], 4 * NEWTON_STEPS * (4 * k + m + 1))
                for t in (2 * m, 2 * m + 1):
                    dve.tensor_scalar(X[:, t, :], X[:, t, :], MV[:, t, 0:1], RS[:, t:t + 1],
                                      ALU.subtract, ALU.mult).then_inc(sm["ln_out"], 1)

            def residual(t):
                dve.wait_ge(sm["gelu_done"], t + 1)
                dve.tensor_tensor(X[:, t, :], X[:, t, :], SM[:, t % 2, :], ALU.add).then_inc(sm["x_added"], 1)
                dve.wait_ge(sm["x_added"], t + 1)
                stats(0, t)

            def by_pos(table, copies, n):
                return table[:, 0:n].unsqueeze(1).broadcast_to([P, copies, n])

            def kv_cos(g):
                dve.wait_ge(sm["kv_act"], g + 1)
                dve.tensor_tensor(KA[:, :].rearrange("p (b k) -> p b k", b=B),
                                  bank[:, VW_BANK, 0:B * KS].rearrange("p (b k) -> p b k", b=B),
                                  by_pos(COS, B, KS), ALU.mult).then_inc(sm["k_cos"], 1)
                ksw = KSW[:, :].rearrange("p (b k) -> p b k", b=B)
                dve.tensor_tensor(ksw, ksw, by_pos(SIN, B, KS), ALU.mult).then_inc(sm["k_sin"], 1)
                lo_part(VTl[:, :], bank[:, VW_BANK, B * KS:2 * B * KS], VTh[:, :]).then_inc(sm["v_lo"], 1)

            def kv_rot(g):
                dve.wait_ge(sm["k_cos"], g + 1)
                dve.wait_ge(sm["k_sin"], g + 1)
                if counted(G * g):
                    dve.wait_ge(sm["s_mm"], G * g)
                ka, ksw = (a[:, :].rearrange("p (a b k) -> p a b k", a=2, b=2) for a in (KA, KSW))
                dve.tensor_tensor(KR[:, :, 0:2, :], ka, ksw, ALU.add)
                dve.tensor_tensor(KR[:, :, 2, :], ka[:, :, 0, :], ksw[:, :, 0, :], ALU.add).then_inc(sm["k_rot"], 1)

            def q_cos(g, h, half):
                i = 2 * G * g + 2 * h + half
                dve.wait_ge(sm["q_swap"], i + 1)
                dve.tensor_tensor(QA[:, half, :].rearrange("p (b s) -> p b s", b=2),
                                  bank[:, Q_BANK + half, :].rearrange("p (b s) -> p b s", b=2),
                                  by_pos(COS, 2, S), ALU.mult).then_inc(sm["q_cos"], 1)

            def q_rot(g, h, half):
                i = 2 * G * g + 2 * h + half
                dve.wait_ge(sm["q_cos"], i + 1)
                dve.wait_ge(sm["q_sin"], i + 1)
                if half == 0:
                    if counted(G * g + h - 1):
                        dve.wait_ge(sm["s_mm"], G * g + h - 1)
                dve.tensor_tensor(QR[:, h % 2, half * HALF:(half + 1) * HALF], QA[:, half, :], QS[:, half, :],
                                  ALU.add).then_inc(sm["q_rot"], 1)

            def sm_rows(h):
                return SM[:, h % 2, :].rearrange("p (t k) -> p t k", k=KS)

            def mask_scores(g, h):
                i = G * g + h
                dve.wait_ge(sm["s_mm"], i + 1)
                if counted(i - 1):
                    dve.wait_ge(sm["p_done"], i - 1)
                dve.scalar_tensor_tensor(out=sm_rows(h), in0=bank[:, S_BANK:S_BANK + 2, :].rearrange("p a (t k) -> p (a t) k", k=P)[:, :, 0:KS],
                                         scalar=1.0 / math.sqrt(DK), in1=MSK[:, :, :], op0=ALU.mult, op1=ALU.add)\
                    .then_inc(sm["s_masked"], 1)

            def row_max(g, h):
                dve.wait_ge(sm["s_masked"], G * g + h + 1)
                dve.tensor_reduce(MX[:, h % 2, :], sm_rows(h), AX_X, ALU.max).then_inc(sm["s_max"], 1)

            def shift(g, h):
                dve.wait_ge(sm["s_max"], G * g + h + 1)
                dve.tensor_tensor(sm_rows(h), sm_rows(h), MX[:, h % 2, :].unsqueeze(2).broadcast_to([P, NT, KS]),
                                  ALU.subtract).then_inc(sm["s_sub"], 1)

            def row_sum(g, h):
                dve.wait_ge(sm["s_exp"], G * g + h + 1)
                dve.tensor_reduce(SU[:, h % 2, :], sm_rows(h), AX_X, ALU.add).then_inc(sm["s_sum"], 1)

            def row_inverse(g, h):
                dve.wait_ge(sm["s_sum"], G * g + h + 1)
                dve.reciprocal(RI[:, h % 2, :], SU[:, h % 2, :]).then_inc(sm["s_inv"], 1)

            def pt_lo(g, pair, part):
                dve.wait_ge(sm["pt_hi"], 4 * g + 2 * pair + part + 1)
                lo_part(PTl[:, pair, part * HALF:(part + 1) * HALF], bank[:, t_bank(part), :],
                        PTh[:, pair, part * HALF:(part + 1) * HALF]).then_inc(sm["pt_lo"], 1)

            def vw_lo(g, u):
                pair, par, bp = u // 4, u // 2 % 2, u % 2
                dve.wait_ge(sm["vw_hi"], 2 * G * g + u + 1)
                for j in range(2):
                    o = (slice(64 * par, 64 * par + 64), pair, 2 * bp + j, slice(0, D))
                    m = lo_part(VWl[o], bank[64 * j:64 * j + 64, vw_bank(u), :], VWh[o])
                m.then_inc(sm["vw_lo"], 1)

            def accumulate(g, t):
                dve.wait_ge(sm["pv_mm"], NT * g + t + 1)
                dve.tensor_tensor(X[:, t, :], X[:, t, :], bank[:, PV_BANK + t % 2, :], ALU.add)\
                    .then_inc(sm["x_added"], 1)

            def group(g, first=False, last=False):
                if first:
                    for t in range(4, NT):
                        x_lo(10 + t, t)
                    kv_cos(g)
                    kv_rot(g)
                    q_cos(g, 0, 0)
                    q_cos(g, 0, 1)
                    q_rot(g, 0, 0)
                    q_rot(g, 0, 1)
                if not first:
                    row_sum(g - 1, 2)
                    pt_lo(g - 1, 0, 0)
                    pt_lo(g - 1, 0, 1)
                    row_inverse(g - 1, 2)
                    q_cos(g, 0, 0)
                    mask_scores(g - 1, 3)
                    q_cos(g, 0, 1)
                    row_max(g - 1, 3)
                    shift(g - 1, 3)
                    q_rot(g, 0, 0)
                    row_sum(g - 1, 3)
                    row_inverse(g - 1, 3)
                q_cos(g, 1, 0)
                if not first:
                    q_rot(g, 0, 1)
                    kv_cos(g)
                q_cos(g, 1, 1)
                if not first:
                    pt_lo(g - 1, 1, 0)
                    kv_rot(g)
                q_rot(g, 1, 0)
                if not first:
                    accumulate(g - 1, 0)
                    pt_lo(g - 1, 1, 1)
                mask_scores(g, 0)
                if not first:
                    accumulate(g - 1, 1)
                    accumulate(g - 1, 2)
                row_max(g, 0)
                shift(g, 0)
                if not first:
                    accumulate(g - 1, 3)
                    accumulate(g - 1, 4)
                q_cos(g, 2, 0)
                if not first:
                    accumulate(g - 1, 5)
                q_rot(g, 1, 1)
                q_rot(g, 2, 0)
                if not first:
                    accumulate(g - 1, 6)
                    accumulate(g - 1, 7)
                vw_lo(g, 0)
                row_sum(g, 0)
                row_inverse(g, 0)
                vw_lo(g, 1)
                q_cos(g, 2, 1)
                mask_scores(g, 1)
                vw_lo(g, 2)
                vw_lo(g, 3)
                row_max(g, 1)
                q_rot(g, 2, 1)
                shift(g, 1)
                vw_lo(g, 4)
                row_sum(g, 1)
                vw_lo(g, 5)
                row_inverse(g, 1)
                vw_lo(g, 6)
                q_cos(g, 3, 0)
                q_cos(g, 3, 1)
                mask_scores(g, 2)
                row_max(g, 2)
                shift(g, 2)
                q_rot(g, 3, 0)
                vw_lo(g, 7)
                q_rot(g, 3, 1)

            for t in range(C):
                dve.wait_ge(sm["w2t_hi"], t + 1)
                w = slice(t * P, (t + 1) * P)
                lo_part(WQl[:, :, w], bank[:, t, :].rearrange("p (c n) -> p c n", n=P), WQh[:, :, w])\
                    .then_inc(sm["w2t_lo"], 1)
            for c in (0, 2):
                dve.wait_ge(sm["w1_hi"], c + 1)
                lo_part(WOl[:, c, :], WOr[:, c, :], WOh[:, c, :]).then_inc(sm["w1_lo_even"], 1)
            x_lo(0, 0)
            x_lo(1, 1)
            dve.wait_ge(sm["b2_hi"], 1)
            lo_part(PTl[0:1, 0, 0:D], QS[0:1, 0, :], PTh[0:1, 0, 0:D]).then_inc(sm["b2_lo"], 1)
            dve.wait_ge(sm["ones_set"], 1)
            dve.tensor_copy(PTh[0:1, 1, 0:P], KA[0:1, 0:P]).then_inc(sm["b2_lo"], 1)
            dve.wait_ge(sm["mask_in"], 16)
            masked(0)
            masked(1)
            x_lo(2, 2)
            masked(2)
            x_lo(3, 3)
            tr_lo(4, CTh[:, 0:2, :], CTl[:, 0:2, :])
            masked(3)
            tr_lo(5, CTh[:, 2:4, :], CTl[:, 2:4, :])
            x_lo(6, 4)
            residual(0)
            x_lo(7, 5)
            residual(1)
            guess(0, 0)
            x_lo(8, 6)
            residual(2)
            x_lo(9, 7)
            normalize(0, 0)
            residual(3)
            guess(0, 1)
            residual(4)
            x_lo(10, 0)
            normalize(0, 1)
            residual(5)
            guess(0, 2)
            x_lo(11, 1)
            residual(6)
            x_lo(12, 2)
            normalize(0, 2)
            x_lo(13, 3)
            residual(7)
            guess(0, 3)
            newton(0, 3)
            normalize(0, 3)
            dve.wait_ge(sm["rope_in"], 32)
            dve.wait_ge(sm["amask_in"], 16)

            group(0, first=True)
            with dve.Fori(1, LAST) as g:
                group(g)
            group(LAST, last=True)

            row_sum(LAST, 2)
            pt_lo(LAST, 0, 0)
            pt_lo(LAST, 0, 1)
            row_inverse(LAST, 2)
            f_hi = [WQh[:, 0, :], WQh[:, 1, :], WQh[:, 2, :], WQh[:, 3, :], WOh[:, 0, :], WOh[:, 1, :]]
            f_lo = [WQl[:, 0, :], WQl[:, 1, :], WQl[:, 2, :], WQl[:, 3, :], WOl[:, 0, :], WOl[:, 1, :]]

            def f_part(j):
                if j < 6:
                    dve.wait_ge(sm["f_hi"], j + 1)
                    m = lo_part(f_lo[j], bank[:, F_BANKS[j], :], f_hi[j])
                else:
                    dve.wait_ge(sm["f_mm"], 7)
                    m = dve.tensor_copy(RWT[:, :, :].rearrange("p c e -> p (c e)"), bank[:, F_BANKS[j], 0:C * E])
                m.then_inc(sm["f_lo"], 1)

            def x2_stats(t):
                dve.wait_ge(sm["x_added"], NT + NT * LAST + t + 1)
                stats(1, t)
                if t % 2:
                    guess(1, t // 2)

            def x2_lo(t):
                a, b = ((ROUTE_FROM, P), (0, P + ROUTE_END))[t % 2]
                dve.wait_ge(sm["tr_hi"], 18 + t + 1)
                dve.tensor_reduce(TS[:, t, :], bank[:, tr_bank(18 + t), :].rearrange("p (c n) -> p c n", n=P)[:, :, a:b],
                                  AX_X, ALU.add).then_inc(sm["tile_sum"], 1)
                x_lo(18 + t, t)

            f_part(0)
            f_part(1)
            mask_scores(LAST, 3)
            row_max(LAST, 3)
            shift(LAST, 3)
            f_part(2)
            row_sum(LAST, 3)
            row_inverse(LAST, 3)
            f_part(3)
            pt_lo(LAST, 1, 0)
            pt_lo(LAST, 1, 1)
            for j in range(4, 7):
                f_part(j)
            accumulate(LAST, 0)
            accumulate(LAST, 1)
            x2_stats(0)
            accumulate(LAST, 2)
            x2_stats(1)
            accumulate(LAST, 3)
            accumulate(LAST, 4)
            x2_stats(2)
            accumulate(LAST, 5)
            normalize(1, 0)
            x2_stats(3)
            accumulate(LAST, 6)
            x2_lo(0)
            x2_lo(1)
            accumulate(LAST, 7)
            x2_stats(4)
            normalize(1, 1)
            x2_stats(5)
            x2_lo(2)
            x2_lo(3)
            x2_stats(6)
            x2_stats(7)
            normalize(1, 2)
            x2_lo(4)
            x2_lo(5)
            normalize(1, 3)
            x2_lo(6)
            x2_lo(7)
            dve.wait_ge(sm["tile_sum"], NT)
            ts = TS[:, :, :].rearrange("p (b i) c -> p i c b", i=TPB)
            dve.tensor_tensor(QT[:, :, :], ts[:, 0, :, :], ts[:, 1, :, :], ALU.add).then_inc(sm["mean_out"], 1)
            dve.wait_ge(sm["lg_mm"], 1)
            dve.wait_ge(sm["rb_in"], 16)
            dve.scalar_tensor_tensor(out=LG[:, 0, :], in0=bank[0:B, LG_BANK, 0:E], scalar=1.0 / (S + ROUTE_END - ROUTE_FROM),
                                     in1=RB[:, :], op0=ALU.mult, op1=ALU.add).then_inc(sm["lg_step"], 1)
            dve.wait_ge(sm["lg_step"], 1)
            dve.tensor_reduce(LS[:, 0:1], LG[:, 0, :], AX_X, ALU.max).then_inc(sm["lg_step"], 1)
            dve.wait_ge(sm["lg_step"], 2)
            dve.tensor_scalar(LG[:, 1, :], LG[:, 0, :], LS[:, 0:1], None, ALU.subtract).then_inc(sm["lg_step"], 1)
            dve.wait_ge(sm["lg_exp"], 1)
            dve.tensor_reduce(LS[:, 1:2], LG[:, 2, :], AX_X, ALU.add).then_inc(sm["lg_step"], 1)
            dve.wait_ge(sm["lg_step"], 4)
            dve.reciprocal(LS[:, 2:3], LS[:, 1:2]).then_inc(sm["lg_step"], 1)
            dve.wait_ge(sm["lg_step"], 5)
            dve.tensor_scalar(R2[:, :].rearrange("p (e r) -> p e r", e=E),
                              LG[:, 2, :].unsqueeze(2).broadcast_to([B, E, R]), LS[:, 2:3], LORA_SCALING,
                              ALU.mult, ALU.mult).then_inc(sm["r_out"], 1)
            dve.wait_ge(sm["rt_mm"], 1)
            dve.tensor_copy(RT[:, :], bank[:, RT_BANK, 0:B]).then_inc(sm["rt_out"], 1)
            for half in range(2):
                dve.wait_ge(sm["ts_hi"], half + 1)
                lo_part(PTl[:, 0, half * HALF:(half + 1) * HALF], QS[:, half, :],
                        PTh[:, 0, half * HALF:(half + 1) * HALF]).then_inc(sm["ts_lo"], 1)
            def out_add(t):
                dve.wait_ge(sm["fy_mm"], t + 1)
                dve.wait_ge(sm["bias_in"], t + 1)
                dve.tensor_tensor(X[:, t, :], X[:, t, :], bank[:, fy_bank(t), :], ALU.add).then_inc(sm["fy_out"], 1)

            def out_stats(t):
                dve.wait_ge(sm["fy_out"], t + 1)
                stats(2, t)
                if t % 2:
                    guess(2, t // 2)

            out_add(0)
            for t in range(1, NT):
                out_add(t)
                out_stats(t - 1)
            out_stats(NT - 1)
            newton(2, 3)
            dve.wait_ge(sm["ln_newton"], 4 * NEWTON_STEPS * (4 * 2 + 4))
            dve.tensor_scalar(NM[:, 6:8], MV[:, 6:8, 0], -1.0, None, ALU.mult).then_inc(sm["last_shift"], 1)
            dve.wait_ge(sm["last_shift"], 1)
            dve.tensor_tensor(NM[:, 6:8], NM[:, 6:8], RS[:, 6:8], ALU.mult).then_inc(sm["last_shift"], 1)
            dve.tensor_scalar(X[:, 6, :], X[:, 6, :], MV[:, 6, 0:1], RS[:, 6:7],
                              ALU.subtract, ALU.mult).then_inc(sm["out_even"], 1)

        @block.gpsimd
        def _(pool):
            def wq_lo(g, h):
                pool.wait_ge(sm["wq_hi"], G * g + h + 1)
                w = slice(h * DK, (h + 1) * DK)
                pool.tensor_tensor(WQl[:, :, w], WQr[:, :, w], f32(WQh[:, :, w]), ALU.subtract)\
                    .then_inc(sm["wq_lo"], 1)

            def wkv_lo(g, i):
                pool.wait_ge(sm["wkv_hi"], g + 1)
                pool.tensor_tensor(KVl[:, i, :, :], KVr[:, i, :, :], f32(KVh[:, i, :, :]), ALU.subtract)\
                    .then_inc(sm["wkv_lo"], 1)

            def wo_lo(g, h):
                pool.wait_ge(sm["wo_hi"], G * g + h + 1)
                pool.tensor_tensor(WOl[:, h, :], WOr[:, h, :], f32(WOh[:, h, :]), ALU.subtract)\
                    .then_inc(sm["wo_lo"], 1)

            def newton(k, m):
                pool.wait_ge(sm["ln_guess"], 3 * (4 * k + m + 1))
                i = 4 * NEWTON_STEPS * (4 * k + m)
                vh, r, w = (a[:, 2 * m:2 * m + 2] for a in (VH, RS, NW))
                for _ in range(NEWTON_STEPS):
                    pool.tensor_tensor(w, r, r, ALU.mult).then_inc(sm["ln_newton"], 1)
                    pool.wait_ge(sm["ln_newton"], i + 1)
                    pool.tensor_tensor(w, w, vh, ALU.mult).then_inc(sm["ln_newton"], 1)
                    pool.wait_ge(sm["ln_newton"], i + 2)
                    pool.tensor_scalar(w, w, 1.5, None, ALU.add).then_inc(sm["ln_newton"], 1)
                    pool.wait_ge(sm["ln_newton"], i + 3)
                    pool.tensor_tensor(r, r, w, ALU.mult).then_inc(sm["ln_newton"], 1)
                    pool.wait_ge(sm["ln_newton"], i + 4)
                    i += 4

            def q_sin(g, h, half):
                pool.wait_ge(sm["q_swap"], 2 * G * g + 2 * h + half + 1)
                q = QS[:, half, :].rearrange("p (b s) -> p b s", b=2)
                pool.tensor_tensor(q, q, SIN[:, :].unsqueeze(1).broadcast_to([P, 2, S]), ALU.mult)\
                    .then_inc(sm["q_sin"], 1)

            def probs(g, h):
                pool.wait_ge(sm["s_inv"], G * g + h + 1)
                if h == 0:
                    if counted(4 * (g - 1) + 2):
                        pool.wait_ge(sm["t_mm"], 4 * (g - 1) + 2)
                if h == 2:
                    pool.wait_ge(sm["t_mm"], 4 * g + 1)
                pool.tensor_tensor(PB[:, h // 2, :, h % 2, :], SM[:, h % 2, :].rearrange("p (t k) -> p t k", k=KS),
                                   RI[:, h % 2, :].unsqueeze(2).broadcast_to([P, NT, KS]), ALU.mult)\
                    .then_inc(sm["p_done"], 1)

            def group(g, first=False, last=False):
                if not first:
                    wo_lo(g, 0)
                q_sin(g, 0, 0)
                if not first:
                    probs(g - 1, 2)
                q_sin(g, 0, 1)
                if not first:
                    probs(g - 1, 3)
                if not last:
                    wq_lo(g + 1, 0)
                q_sin(g, 1, 0)
                if not last:
                    wkv_lo(g + 1, 0)
                if not first:
                    wo_lo(g, 1)
                if not first:
                    wo_lo(g, 2)
                q_sin(g, 1, 1)
                q_sin(g, 2, 0)
                if not first:
                    wo_lo(g, 3)
                probs(g, 0)
                if not last:
                    wq_lo(g + 1, 1)
                q_sin(g, 2, 1)
                probs(g, 1)
                if not last:
                    wq_lo(g + 1, 2)
                q_sin(g, 3, 0)
                q_sin(g, 3, 1)
                if not last:
                    wq_lo(g + 1, 3)
                    wkv_lo(g + 1, 1)

            pool.memset(ID[:, :], 0.0).then_inc(sm["ident"], 1)
            pool.wait_ge(sm["ident"], 1)
            pool.affine_select(out=ID[:, :], in_=ID[:, :], compare_op=ALU.not_equal, fill=1.0, base=0,
                               pattern=[[-1, P]], channel_multiplier=1).then_inc(sm["ident"], 1)
            pool.memset(KA[0:1, 0:P], 1.0).then_inc(sm["ones_set"], 1)
            for c in (1, 3):
                pool.wait_ge(sm["w1_hi"], c + 1)
                pool.tensor_tensor(WOl[:, c, :], WOr[:, c, :], f32(WOh[:, c, :]), ALU.subtract)\
                    .then_inc(sm["w1_lo_odd"], 1)
            wq_lo(0, 0)
            wkv_lo(0, 0)
            wkv_lo(0, 1)
            wq_lo(0, 1)
            newton(0, 0)
            wo_lo(0, 0)
            wo_lo(0, 1)
            newton(0, 1)
            wo_lo(0, 2)
            wo_lo(0, 3)
            newton(0, 2)
            wq_lo(0, 2)
            wq_lo(0, 3)
            pool.wait_ge(sm["rope_in"], 32)

            group(0, first=True)
            with pool.Fori(1, LAST) as g:
                group(g)
            group(LAST, last=True)

            probs(LAST, 2)
            probs(LAST, 3)
            for m in range(4):
                newton(1, m)
            pool.wait_ge(sm["fb_in"], 16)
            for t in range(NT):
                pool.wait_ge(sm["tr_mm"], 18 + t + 1)
                pool.tensor_tensor(X[:, t, :], X[:, t, :], WOr[:, 3, :], ALU.add).then_inc(sm["bias_in"], 1)
            for m in range(3):
                newton(2, m)
                pair = slice(2 * m, 2 * m + 2)
                pool.tensor_tensor(NM[:, pair], MV[:, pair, 0], RS[:, pair], ALU.mult).then_inc(sm["ln_shift"], 1)
                pool.wait_ge(sm["ln_shift"], 2 * m + 1)
                pool.tensor_scalar(NM[:, pair], NM[:, pair], -1.0, None, ALU.mult).then_inc(sm["ln_shift"], 1)


_INS = ['x', 'ctx_4096', 'mask_BxSxS2_ff0', 'L0_attn_w1', 'L0_attn_w2', 'L0_attn_b2', 'L0_attn_sparse_mask', 'L0_xattn_wq', 'L0_xattn_wk',
        'L0_xattn_wv', 'L0_xattn_wo', 'L0_ffn_W', 'L0_ffn_b', 'L0_ffn_A', 'L0_ffn_B', 'L0_ffn_router_W', 'L0_ffn_router_b']


def kernel(**inputs):
    import numpy as _np
    import concourse.bacc as _bacc
    from concourse import mybir as _mybir
    from concourse.bass_utils import run_bass_kernel_spmd as _run

    nc = _bacc.Bacc("TRN2", target_bir_lowering=False, num_devices=1)
    b, s, d = inputs["x"].shape
    arrays, args = {}, []
    given = [(n, inputs[n]) for n in _INS] + [("rope", rope_tables(P, s))]
    for name, a in given:
        a = _np.ascontiguousarray(a)
        arrays[f"in_{name}_dram"] = a
        args.append(nc.dram_tensor(f"in_{name}_dram", a.shape, _mybir.dt.from_np(a.dtype), kind="ExternalInput").ap())
    args.append(nc.dram_tensor("out_0_dram", (b, s, d), F32, kind="ExternalOutput").ap())
    decoder_layer(nc, *args)
    r = _run(nc, [arrays], core_ids=[0])
    return r.results[0]["out_0_dram"]
```

```python
from contextlib import ExitStack
import math

import numpy as np

import concourse.bass as bass
from concourse import mybir

F32 = mybir.dt.float32
F32R = mybir.dt.float32r
I32 = mybir.dt.int32
ACT = mybir.ActivationFunctionType
ALU = mybir.AluOpType
AX_X = mybir.AxisListType.X

P = 128
LN_EPS = 1e-5
RSQRT_GUESS = float(0x5F3759DF)
NEWTON_STEPS = 3
ROUTE_FROM, ROUTE_END = 107, -1
LORA_SCALING = 2.0


def rope_tables(dk, positions):
    inv_freq = (1.0 / np.float32(10000.0) ** (np.arange(0, dk, 2, dtype=np.float32) / np.float32(dk))).astype(np.float32)
    ang = inv_freq[:, None] * np.arange(positions, dtype=np.float32)[None, :]
    cos, sin = np.cos(ang), np.sin(ang)
    return np.stack([np.concatenate([cos, cos]), np.concatenate([-sin, sin])]).astype(np.float32)


def decoder_layer(nc, x, ctx_in, amask, w1, w2, b2, smask, wq, wk, wv, wo, fW, fb, fA, fB, rW, rb, rope, out):
    B, S, D = x.shape
    KS = ctx_in.shape[1]
    HQ, DK = wq.shape[1] // P, P
    HKV = wk.shape[1] // P
    G = HQ // HKV
    E, R = fA.shape[0], fA.shape[1]
    C = D // P
    NT = B * S // P
    TPB = S // P
    HALF = 512
    assert (B, S, D, KS, G, E * R) == (4, 256, 512, 64, 4, 128)

    x_v = x.rearrange("b s d -> (b s) d").rearrange("(t p) d -> p t d", p=P)
    out_v = out.rearrange("b s d -> (b s) d").rearrange("(t p) d -> p t d", p=P)
    amask_v = amask.rearrange("b s k -> (b s) k").rearrange("(t p) k -> p t k", p=P)
    ctx_v = ctx_in.rearrange("b s d -> (b s) d").rearrange("(t p) d -> p t d", p=P)

    def rows(a):
        return a.rearrange("(c p) n -> p c n", p=P)

    with ExitStack() as es:
        def sb(name, shape, dt=F32):
            return es.enter_context(nc.sbuf_tensor(name, shape, dt))

        def sem(name):
            return es.enter_context(nc.semaphore(name))

        X = sb("X", [P, NT, D])
        XTh, XTl = (sb(f"XT{s}", [P, C, B * S], F32R) for s in "hl")
        VWh, VWl = (sb(f"VW{s}", [P, 2, B, D], F32R) for s in "hl")
        WQr = sb("WQr", [P, C, G * DK])
        WQh, WQl = (sb(f"WQ{s}", [P, C, G * DK], F32R) for s in "hl")
        WOr = sb("WOr", [P, G, D])
        WOh, WOl = (sb(f"WO{s}", [P, G, D], F32R) for s in "hl")
        KVr = sb("KVr", [P, 2, C, DK])
        KVh, KVl = (sb(f"KV{s}", [P, 2, C, DK], F32R) for s in "hl")
        CTh, CTl = (sb(f"CT{s}", [P, C, B * KS], F32R) for s in "hl")
        KR = sb("KR", [P, 2, 3, KS])
        KSW = sb("KSW", [P, B * KS])
        KA = sb("KA", [P, B * KS])
        VTh, VTl = (sb(f"VT{s}", [P, B * KS], F32R) for s in "hl")
        QR = sb("QR", [P, 2, B * S])
        QS = sb("QS", [P, 2, HALF])
        QA = sb("QA", [P, 2, HALF])
        PB = sb("PB", [P, 2, NT, 2, KS])
        SM = sb("SM", [P, 2, NT * KS])
        PTh, PTl = (sb(f"PT{s}", [P, 2, B * S], F32R) for s in "hl")
        MSK = sb("MSK", [P, NT, KS])
        COS = sb("COS", [P, S])
        SIN = sb("SIN", [P, S])
        ID = sb("ID", [P, P])
        MX = sb("MX", [P, 2, NT])
        SU = sb("SU", [P, 2, NT])
        RI = sb("RI", [P, 2, NT])
        BST = sb("BST", [P, 2, 6])
        MV = sb("MV", [P, NT, 2])
        VE = sb("VE", [P, NT])
        RS = sb("RS", [P, NT])
        NW = sb("NW", [P, NT])
        NM = sb("NM", [P, NT])
        VH = sb("VH", [P, NT])
        TS = sb("TS", [P, NT, C])
        QT = sb("QT", [P, C, B])
        RWT = sb("RWT", [P, C, E])
        RB = sb("RB", [B, E])
        LG = sb("LG", [B, 4, E])
        LS = sb("LS", [B, 4])
        R2 = sb("R2", [B, E * R])
        RT = sb("RT", [P, B])

        bank = es.enter_context(nc.psum_tensor("bank", [P, 8, 512], F32))
        Q_BANK, S_BANK, T_BANK, VW_BANK, PV_BANK = 0, 2, 4, 5, 6

        names = """mask_in ctx_in_ b2_in rope_in wq_in wo_in wk_in wv_in fw_in fa_in fbm_in rw_in rb_in
        fb_in amask_in stored ident ones_set w2t_mm w2t_hi w2t_lo w1_hi w1_lo_even w1_lo_odd b2_hi b2_lo tr_mm tr_hi tr_lo
        at_mm at_masked at_hi at_lo y_mm gelu_done x_added ln_stats ln_mean ln_guess ln_newton ln_out ln_shift last_shift out_done out_even
        wq_hi wq_lo wo_hi wo_lo wkv_hi wkv_lo kv_mm kv_act k_cos k_sin k_rot v_lo
        q_mm q_swap q_cos q_sin q_rot s_mm s_masked s_max s_sub s_exp s_sum s_inv p_done
        t_mm pt_hi pt_lo vw_mm vw_hi vw_lo pv_mm
        f_mm f_hi f_lo tile_sum mean_out lg_mm lg_step lg_exp r_out rt_mm rt_out tt_mm ts_out ts_hi ts_lo
        fy_mm fy_out bias_in""".split()
        sm = {n: sem(n) for n in names}
        x_in = [sem(f"x_in{i}") for i in range(5)]
        w1_in, w2_in = ([sem(f"{w}_in{c}") for c in range(C)] for w in ("w1", "w2"))

        def counted(value):
            return not isinstance(value, int) or value > 0

        SMASK = PB[:, :, :, :, :].rearrange("p i t a k -> p (i t a k)").rearrange("p (c n) -> p c n", n=D)
        block = es.enter_context(nc.Block())
        f32 = lambda ap: ap.bitcast(F32)

        def vw_bank(u):
            return (T_BANK, VW_BANK)[u % 2]

        def t_bank(part):
            return (T_BANK, PV_BANK + 1)[part]

        def tr_bank(n):
            return (S_BANK if n in (16, 17, 18, 19) else PV_BANK) + n % 2

        def y_bank(t):
            return 2 + t % 2

        def fy_bank(t):
            return (0, 1, 2, 3, 6, 7, 0, 1)[t]

        F_BANKS = (6, 0, 1, 5, 0, 1, 5)
        LORA_BANK, LG_BANK, RT_BANK = 4, 7, 7
        LAST = HKV - 1

        @block.sync
        def _(sp):
            def load(dst, src, name):
                sp.dma_start(dst, src).then_inc(sm[name], 16)

            for c in range(C):
                sp.dma_start(WQr[:, c, :], rows(w2)[:, c, :]).then_inc(w2_in[c], 16)
            for c in range(C):
                sp.dma_start(WOr[:, c, :], rows(w1)[:, c, :]).then_inc(w1_in[c], 16)
            for i in range(2):
                sp.dma_start(X[:, i, :], x_v[:, i, :]).then_inc(x_in[i], 16)
            load(SMASK, rows(smask), "mask_in")
            sp.dma_start(X[:, 2:4, :], x_v[:, 2:4, :]).then_inc(x_in[2], 16)
            load(QR[:, :, 0:D], ctx_v, "ctx_in_")
            load(QS[0:1, 0, :], b2.rearrange("(a n) -> a n", a=1), "b2_in")
            for i in (2, 3):
                sp.dma_start(X[:, 2 * i:2 * i + 2, :], x_v[:, 2 * i:2 * i + 2, :]).then_inc(x_in[i + 1], 16)
            load(KVr[:, 0, :, :], rows(wk)[:, :, 0:DK], "wk_in")
            load(KVr[:, 1, :, :], rows(wv)[:, :, 0:DK], "wv_in")
            load(COS[:, :], rope[0, :, :], "rope_in")
            load(SIN[:, :], rope[1, :, :], "rope_in")
            load(MSK[:, :, :], amask_v, "amask_in")
            load(RB[:, :], rb.rearrange("(a n) -> a n", a=1).broadcast_to([B, E]), "rb_in")
            sp.wait_ge(sm["w2t_mm"], C)
            load(WQr[:, :, :], rows(wq)[:, :, 0:G * DK], "wq_in")
            sp.wait_ge(sm["w1_lo_even"], 2)
            sp.wait_ge(sm["w1_lo_odd"], 2)
            load(WOr[:, :, :], rows(wo[0:G * DK, :]), "wo_in")
            with sp.Fori(1, HKV) as g:
                kv_at, q_at = sp.snap(g * DK), sp.snap(g * G * DK)
                sp.wait_ge(sm["wkv_lo"], 2 * g)
                load(KVr[:, 0, :, :], rows(wk)[:, :, bass.ds(kv_at, DK)], "wk_in")
                load(KVr[:, 1, :, :], rows(wv)[:, :, bass.ds(kv_at, DK)], "wv_in")
                sp.wait_ge(sm["wq_lo"], g * G)
                load(WQr[:, :, :], rows(wq)[:, :, bass.ds(q_at, G * DK)], "wq_in")
                sp.wait_ge(sm["wo_lo"], g * G)
                load(WOr[:, :, :], rows(wo[bass.ds(q_at, G * DK), :]), "wo_in")
            sp.wait_ge(sm["wq_lo"], HKV * G)
            load(WQr[:, :, :], rows(fW), "fw_in")
            sp.wait_ge(sm["wo_lo"], HKV * G)
            load(WOr[:, 0, :], fA.rearrange("e r d -> (e r) d"), "fa_in")
            for oc in range(C):
                load(WOr[:, 1, oc * P:(oc + 1) * P].rearrange("p (e r) -> p e r", e=E),
                     fB[:, oc * P:(oc + 1) * P, :].rearrange("e p r -> p e r"), "fbm_in")
            load(WOr[0:E, 2, :], rW, "rw_in")
            load(WOr[:, 3, :], fb.rearrange("(a n) -> a n", a=1).broadcast_to([P, D]), "fb_in")
            for t in range(NT):
                if t == 6:
                    sp.wait_ge(sm["out_even"], 1)
                else:
                    sp.wait_ge(sm["out_done"], min(t + 1, 7))
                load(out_v[:, t, :], X[:, t, :], "stored")
            sp.wait_ge(sm["stored"], 16 * NT)

        @block.tensor
        def _(pe):
            def mm3(o, lh, ll, rh, rl, start=True, stop=True):
                pe.matmul(o, lh, rh, start=start, stop=False)
                pe.matmul(o, lh, rl, start=False, stop=False)
                return pe.matmul(o, ll, rh, start=False, stop=stop)

            def transpose_tile(n, tiles):
                if n < 16 or n >= 22:
                    if counted(n - 1):
                        pe.wait_ge(sm["tr_lo"], n - 1)
                for out_at, src in tiles:
                    m = pe.transpose(bank[:, tr_bank(n), out_at:out_at + P], src, ID[:, :])
                m.then_inc(sm["tr_mm"], 1)

            def x_tile(n, t):
                transpose_tile(n, [(c * P, X[:, t, c * P:(c + 1) * P]) for c in range(C)])

            def attn_weights(s):
                for c in range(C):
                    if s == 0:
                        pe.wait_ge(sm[("w1_lo_even", "w1_lo_odd")[c % 2]], c // 2 + 1)
                    m = mm3(bank[:, (4, 5, 0, 1)[s], :], WOh[:, c, s * P:(s + 1) * P], WOl[:, c, s * P:(s + 1) * P],
                            WQh[:, c, :], WQl[:, c, :], start=c == 0, stop=c == C - 1)
                m.then_inc(sm["at_mm"], 1)

            def dense(t):
                pe.wait_ge(sm["tr_lo"], t + 1 + (2 if t > 3 else 0))
                if counted(t - 1):
                    pe.wait_ge(sm["gelu_done"], t - 1)
                o = bank[:, y_bank(t), :]
                pe.matmul(o, PTh[0:1, 1, 0:P], PTh[0:1, 0, 0:D], start=True, stop=False)
                pe.matmul(o, PTh[0:1, 1, 0:P], PTl[0:1, 0, 0:D], start=False, stop=False)
                for s in range(C):
                    if t == 0:
                        pe.wait_ge(sm["at_lo"], s + 1)
                    m = mm3(o, XTh[:, s, t * P:(t + 1) * P], XTl[:, s, t * P:(t + 1) * P],
                            VWh[:, 0, s, :], VWl[:, 0, s, :], start=False, stop=s == C - 1)
                m.then_inc(sm["y_mm"], 1)

            def keys(g):
                pe.wait_ge(sm["wkv_lo"], 2 * g + 1)
                if counted(2 * G * g):
                    pe.wait_ge(sm["vw_lo"], 2 * G * g)
                for c in range(C):
                    mm3(bank[:, VW_BANK, 0:B * KS], KVh[:, 0, c, :], KVl[:, 0, c, :], CTh[:, c, :], CTl[:, c, :],
                        start=c == 0, stop=c == C - 1)

            def values(g):
                pe.wait_ge(sm["wkv_lo"], 2 * g + 2)
                for c in range(C):
                    m = mm3(bank[:, VW_BANK, B * KS:2 * B * KS], KVh[:, 1, c, :], KVl[:, 1, c, :],
                            CTh[:, c, :], CTl[:, c, :], start=c == 0, stop=c == C - 1)
                m.then_inc(sm["kv_mm"], 1)

            def query(g, h, half):
                pe.wait_ge(sm["wq_lo"], G * g + h + 1)
                if counted(2 * G * g + 2 * h + half - 1):
                    pe.wait_ge(sm["q_cos"], 2 * G * g + 2 * h + half - 1)
                for c in range(C):
                    m = mm3(bank[:, Q_BANK + half, :], WQh[:, c, h * DK:(h + 1) * DK], WQl[:, c, h * DK:(h + 1) * DK],
                            XTh[:, c, half * HALF:(half + 1) * HALF], XTl[:, c, half * HALF:(half + 1) * HALF],
                            start=c == 0, stop=c == C - 1)
                m.then_inc(sm["q_mm"], 1)

            def scores(g, h):
                pe.wait_ge(sm["q_rot"], 2 * G * g + 2 * h + 2)
                pe.wait_ge(sm["k_rot"], g + 1)
                if counted(G * g + h):
                    pe.wait_ge(sm["s_masked"], G * g + h)
                for t in range(NT):
                    b = t // TPB
                    m = pe.matmul(bank[:, S_BANK + t // 4, t % 4 * P:(t % 4 + 1) * P], QR[:, h % 2, t * P:(t + 1) * P],
                                  KR[:, b // 2, b % 2:b % 2 + 2, :].rearrange("p b k -> p (b k)"), start=True, stop=True)
                m.then_inc(sm["s_mm"], 1)

            def probs_transpose(g, pair, part):
                pe.wait_ge(sm["p_done"], G * g + 2 * pair + 2)
                if counted(4 * g + 2 * pair + part - 1):
                    pe.wait_ge(sm["pt_lo"], 4 * g + 2 * pair + part - 1)
                if pair == 0 and part == 0:
                    pe.wait_ge(sm["vw_lo"], 2 * G * g + 7)
                elif pair == 0:
                    pe.wait_ge(sm["x_added"], NT + NT * g)
                for j in range(4):
                    m = pe.transpose(bank[:, t_bank(part), j * P:(j + 1) * P],
                                     PB[:, pair, 4 * part + j, :, :].rearrange("p a k -> p (a k)"), ID[:, :])
                m.then_inc(sm["t_mm"], 1)

            def value_out(g, u):
                pair, par, bp = u // 4, u // 2 % 2, u % 2
                h = 2 * pair + par
                pe.wait_ge(sm["wo_lo"], G * g + h + 1)
                pe.wait_ge(sm["v_lo"], g + 1)
                if counted(2 * G * g + u - 1):
                    pe.wait_ge(sm["vw_lo"], 2 * G * g + u - 1)
                mm3(bank[:, vw_bank(u), :], VTh[:, bp * P:(bp + 1) * P], VTl[:, bp * P:(bp + 1) * P],
                    WOh[:, h, :], WOl[:, h, :]).then_inc(sm["vw_mm"], 1)

            def attend(g, t):
                pe.wait_ge(sm["pt_lo"], 4 * g + (3 if t == 0 else 4))
                pe.wait_ge(sm["vw_lo"], 2 * G * (g + 1))
                pe.wait_ge(sm["x_added"], NT + NT * g + t - 1)
                for pair in range(2):
                    m = mm3(bank[:, PV_BANK + t % 2, :], PTh[:, pair, t * P:(t + 1) * P], PTl[:, pair, t * P:(t + 1) * P],
                            VWh[:, pair, t // TPB, :], VWl[:, pair, t // TPB, :], start=pair == 0, stop=pair == 1)
                m.then_inc(sm["pv_mm"], 1)

            def group(g, first=False):
                if first:
                    for t in range(4, NT):
                        pe.wait_ge(sm["ln_out"], t + 1)
                        pe.wait_ge(sm["gelu_done"], t + 1)
                        x_tile(10 + t, t)
                        if t == 4:
                            keys(g)
                            values(g)
                            pe.wait_ge(sm["tr_lo"], 14)
                            query(g, 0, 0)
                    pe.wait_ge(sm["tr_lo"], 18)
                    query(g, 0, 1)
                if not first:
                    query(g, 0, 0)
                    query(g, 0, 1)
                    keys(g)
                    scores(g - 1, 3)
                    values(g)
                query(g, 1, 0)
                query(g, 1, 1)
                if not first:
                    probs_transpose(g - 1, 1, 0)
                    probs_transpose(g - 1, 1, 1)
                query(g, 2, 0)
                if not first:
                    attend(g - 1, 0)
                scores(g, 0)
                if not first:
                    for t in range(1, 4):
                        attend(g - 1, t)
                value_out(g, 0)
                if not first:
                    for t in range(4, 8):
                        attend(g - 1, t)
                value_out(g, 1)
                query(g, 2, 1)
                value_out(g, 2)
                scores(g, 1)
                value_out(g, 3)
                query(g, 3, 0)
                value_out(g, 4)
                value_out(g, 5)
                query(g, 3, 1)
                value_out(g, 6)
                scores(g, 2)
                value_out(g, 7)
                probs_transpose(g, 0, 0)
                probs_transpose(g, 0, 1)

            pe.wait_ge(sm["ident"], 2)
            for t in range(C):
                pe.wait_ge(w2_in[t], 16)
                for c in range(C):
                    m = pe.transpose(bank[:, t, c * P:(c + 1) * P], WQr[:, t, c * P:(c + 1) * P], ID[:, :])
                m.then_inc(sm["w2t_mm"], 1)
            pe.wait_ge(sm["w2t_lo"], C)
            attn_weights(0)
            for t in range(2):
                pe.wait_ge(x_in[t], 16)
                x_tile(t, t)
            attn_weights(1)
            pe.wait_ge(x_in[2], 16)
            x_tile(2, 2)
            attn_weights(2)
            x_tile(3, 3)
            attn_weights(3)
            pe.wait_ge(sm["ctx_in_"], 16)
            for n in range(2):
                transpose_tile(4 + n, [(256 * j + r * P, QR[:, r, (2 * n + j) * P:(2 * n + j + 1) * P])
                                       for j in range(2) for r in range(2)])
            pe.wait_ge(sm["b2_lo"], 2)
            dense(0)
            pe.wait_ge(x_in[3], 16)
            x_tile(6, 4)
            dense(1)
            x_tile(7, 5)
            dense(2)
            pe.wait_ge(x_in[4], 16)
            x_tile(8, 6)
            dense(3)
            x_tile(9, 7)
            dense(4)
            pe.wait_ge(sm["ln_out"], 2)
            x_tile(10, 0)
            dense(5)
            x_tile(11, 1)
            dense(6)
            pe.wait_ge(sm["ln_out"], 4)
            x_tile(12, 2)
            dense(7)
            x_tile(13, 3)

            group(0, first=True)
            with pe.Fori(1, LAST) as g:
                group(g)

            def weight_transpose(j):
                if j == 0:
                    pe.wait_ge(sm["x_added"], NT + NT * LAST - 1)
                elif j < 3:
                    pe.wait_ge(sm["q_cos"], 2 * G * HKV - 2 + j)
                elif j == 3:
                    pe.wait_ge(sm["vw_lo"], 2 * G * HKV)
                else:
                    pe.wait_ge(sm["f_lo"], j - 2)
                for name, first, value in (("fw_in", 0, 16), ("fa_in", 4, 16), ("fbm_in", 5, 16 * C), ("rw_in", 6, 16)):
                    if j == first:
                        pe.wait_ge(sm[name], value)
                o = bank[:, F_BANKS[j], :]
                for t in range(C):
                    src = WQr[:, t, j * P:(j + 1) * P] if j < 4 else WOr[:, j - 4, t * P:(t + 1) * P]
                    if j == 6:
                        m = pe.transpose(o[:, t * E:(t + 1) * E], src[0:E, :], ID[0:E, 0:E])
                    else:
                        m = pe.transpose(o[:, t * P:(t + 1) * P], src, ID[:, :])
                m.then_inc(sm["f_mm"], 1)

            def x2_tile(t):
                pe.wait_ge(sm["ln_out"], NT + t + 1)
                if t < 2:
                    pe.wait_ge(sm["s_masked"], G * HKV)
                elif t < 4:
                    pe.wait_ge(sm["x_added"], NT + NT * HKV - 3 + t)
                x_tile(18 + t, t)

            def lora_in(half):
                pe.wait_ge(sm["tr_lo"], 18 + 4 * (half + 1))
                pe.wait_ge(sm["f_lo"], 5)
                if half == 0:
                    pe.wait_ge(sm["pt_lo"], 4 * HKV - 1)
                else:
                    pe.wait_ge(sm["f_lo"], 7)
                for c in range(C):
                    m = mm3(bank[:, LORA_BANK + half, :], WOh[:, 0, c * P:(c + 1) * P], WOl[:, 0, c * P:(c + 1) * P],
                            XTh[:, c, half * HALF:(half + 1) * HALF], XTl[:, c, half * HALF:(half + 1) * HALF],
                            start=c == 0, stop=c == C - 1)
                m.then_inc(sm["tt_mm"], 1)

            def base(t):
                if t < 2:
                    pe.wait_ge(sm["f_lo"], 5 + t)
                elif t < 4:
                    pe.wait_ge(sm["tr_lo"], 17 + t)
                elif t == 4:
                    pe.wait_ge(sm["tr_lo"], 25)
                elif t == 5:
                    pe.wait_ge(sm["rt_out"], 1)
                else:
                    pe.wait_ge(sm["fy_out"], t - 5)
                pe.wait_ge(sm["tr_lo"], 18 + t + 1)
                for c in range(C):
                    mm3(bank[:, fy_bank(t), :], XTh[:, c, t * P:(t + 1) * P], XTl[:, c, t * P:(t + 1) * P],
                        WQh[:, c, :], WQl[:, c, :], start=c == 0, stop=False)

            def lora_out(t):
                pe.wait_ge(sm["ts_lo"], t // 4 + 1)
                pe.wait_ge(sm["f_lo"], 6)
                mm3(bank[:, fy_bank(t), :], PTh[:, 0, t * P:(t + 1) * P], PTl[:, 0, t * P:(t + 1) * P],
                    WOh[:, 1, :], WOl[:, 1, :], start=False, stop=True).then_inc(sm["fy_mm"], 1)

            def logits():
                pe.wait_ge(sm["mean_out"], 1)
                pe.wait_ge(sm["f_lo"], 7)
                for c in range(C):
                    m = pe.matmul(bank[0:B, LG_BANK, 0:E], QT[:, c, :], RWT[:, c, :], start=c == 0, stop=c == C - 1)
                m.then_inc(sm["lg_mm"], 1)

            def route_transpose():
                pe.wait_ge(sm["r_out"], 1)
                pe.transpose(bank[:, RT_BANK, 0:B], R2[:, :], ID[0:B, 0:B]).then_inc(sm["rt_mm"], 1)

            query(LAST, 0, 0)
            query(LAST, 0, 1)
            scores(LAST - 1, 3)
            keys(LAST)
            query(LAST, 1, 0)
            values(LAST)
            query(LAST, 1, 1)
            probs_transpose(LAST - 1, 1, 0)
            probs_transpose(LAST - 1, 1, 1)
            query(LAST, 2, 0)
            scores(LAST, 0)
            for i in range(0, 4):
                attend(LAST - 1, i)
            value_out(LAST, 0)
            scores(LAST, 1)
            for i in range(4, 8):
                attend(LAST - 1, i)
            value_out(LAST, 1)
            query(LAST, 2, 1)
            value_out(LAST, 2)
            value_out(LAST, 3)
            query(LAST, 3, 0)
            value_out(LAST, 4)
            query(LAST, 3, 1)
            scores(LAST, 2)
            value_out(LAST, 5)
            value_out(LAST, 6)
            scores(LAST, 3)
            weight_transpose(0)
            probs_transpose(LAST, 0, 0)
            weight_transpose(1)
            value_out(LAST, 7)
            probs_transpose(LAST, 0, 1)
            weight_transpose(2)
            probs_transpose(LAST, 1, 0)
            probs_transpose(LAST, 1, 1)
            weight_transpose(3)
            pe.wait_ge(sm["f_lo"], 1)
            for i in range(0, 3):
                attend(LAST, i)
            weight_transpose(4)
            attend(LAST, 3)
            attend(LAST, 4)
            weight_transpose(5)
            attend(LAST, 5)
            attend(LAST, 6)
            x2_tile(0)
            attend(LAST, 7)
            x2_tile(1)
            base(0)
            x2_tile(2)
            base(1)
            x2_tile(3)
            base(2)
            x2_tile(4)
            x2_tile(5)
            lora_in(0)
            x2_tile(6)
            x2_tile(7)
            weight_transpose(6)
            base(3)
            logits()
            base(4)
            route_transpose()
            lora_in(1)
            for i in range(0, 3):
                lora_out(i)
            base(5)
            lora_out(3)
            base(6)
            lora_out(4)
            lora_out(5)
            base(7)
            lora_out(6)
            lora_out(7)

        @block.scalar
        def _(act):
            def copy(o, i):
                return act.activation(o, i, ACT.Copy)

            def tr_hi(n, dst):
                act.wait_ge(sm["tr_mm"], n + 1)
                copy(dst, bank[:, tr_bank(n), :].rearrange("p (c n) -> p c n", n=dst.shape[-1]))\
                    .then_inc(sm["tr_hi"], 1)

            def x_hi(n, t):
                tr_hi(n, XTh[:, :, t * P:(t + 1) * P])

            def gelu(t):
                act.wait_ge(sm["y_mm"], t + 1)
                if counted(t - 1):
                    act.wait_ge(sm["x_added"], t - 1)
                act.activation(SM[:, t % 2, :], bank[:, y_bank(t), :], ACT.Gelu).then_inc(sm["gelu_done"], 1)

            def wq_hi(g, h):
                act.wait_ge(sm["wq_in"], 16 * (g + 1))
                if counted(2 * G * (g - 1) + 2 * h + 2):
                    act.wait_ge(sm["q_mm"], 2 * G * (g - 1) + 2 * h + 2)
                copy(WQh[:, :, h * DK:(h + 1) * DK], WQr[:, :, h * DK:(h + 1) * DK]).then_inc(sm["wq_hi"], 1)

            def wo_hi(g):
                act.wait_ge(sm["wo_in"], 16 * (g + 1))
                if counted(2 * G * g):
                    act.wait_ge(sm["vw_mm"], 2 * G * g)
                if isinstance(g, int) and g == 0:
                    act.wait_ge(sm["at_mm"], C)
                for h in range(G):
                    copy(WOh[:, h, :], WOr[:, h, :]).then_inc(sm["wo_hi"], 1)

            def wkv_hi(g):
                act.wait_ge(sm["wk_in"], 16 * (g + 1))
                act.wait_ge(sm["wv_in"], 16 * (g + 1))
                if counted(g):
                    act.wait_ge(sm["kv_mm"], g)
                copy(KVh[:, :, :, :], KVr[:, :, :, :]).then_inc(sm["wkv_hi"], 1)

            def kv(g):
                act.wait_ge(sm["kv_mm"], g + 1)
                if counted(g):
                    act.wait_ge(sm["k_rot"], g)
                if counted(2 * G * g):
                    act.wait_ge(sm["vw_mm"], 2 * G * g)
                for lo, hi in ((0, 64), (64, 0)):
                    copy(KSW[lo:lo + 64, :], bank[hi:hi + 64, VW_BANK, 0:B * KS])
                copy(VTh[:, :], bank[:, VW_BANK, B * KS:2 * B * KS]).then_inc(sm["kv_act"], 1)

            def swap(g, h, half):
                i = 2 * G * g + 2 * h + half
                act.wait_ge(sm["q_mm"], i + 1)
                if counted(i - 1):
                    act.wait_ge(sm["q_rot"], i - 1)
                for lo, hi in ((0, 64), (64, 0)):
                    m = copy(QS[lo:lo + 64, half, :], bank[hi:hi + 64, Q_BANK + half, :])
                m.then_inc(sm["q_swap"], 1)

            def exps(g, h):
                act.wait_ge(sm["s_sub"], G * g + h + 1)
                act.activation(SM[:, h % 2, :], SM[:, h % 2, :], ACT.Exp)\
                    .then_inc(sm["s_exp"], 1)

            def pt_hi(g, pair, part):
                act.wait_ge(sm["t_mm"], 4 * g + 2 * pair + part + 1)
                if pair == 0 and part == 0:
                    if counted(NT * g):
                        act.wait_ge(sm["pv_mm"], NT * g)
                copy(PTh[:, pair, part * HALF:(part + 1) * HALF], bank[:, t_bank(part), :]).then_inc(sm["pt_hi"], 1)

            def vw_hi(g, u):
                pair, par, bp = u // 4, u // 2 % 2, u % 2
                act.wait_ge(sm["vw_mm"], 2 * G * g + u + 1)
                if u == 0:
                    if counted(NT * g):
                        act.wait_ge(sm["pv_mm"], NT * g)
                for j in range(2):
                    m = copy(VWh[64 * par:64 * par + 64, pair, 2 * bp + j, :], bank[64 * j:64 * j + 64, vw_bank(u), :])
                m.then_inc(sm["vw_hi"], 1)

            def group(g, first=False, last=False):
                if first:
                    x_hi(14, 4)
                    kv(g)
                    for t in range(5, NT):
                        x_hi(10 + t, t)
                    swap(g, 0, 0)
                    swap(g, 0, 1)
                if not first:
                    swap(g, 0, 0)
                    swap(g, 0, 1)
                if not first:
                    wo_hi(g)
                if not first:
                    kv(g)
                    exps(g - 1, 3)
                if not last:
                    wq_hi(g + 1, 0)
                swap(g, 1, 0)
                swap(g, 1, 1)
                if not first:
                    pt_hi(g - 1, 1, 0)
                if not last:
                    wkv_hi(g + 1)
                if not first:
                    pt_hi(g - 1, 1, 1)
                swap(g, 2, 0)
                exps(g, 0)
                vw_hi(g, 0)
                vw_hi(g, 1)
                if not last:
                    wq_hi(g + 1, 1)
                swap(g, 2, 1)
                for i in range(2, 5):
                    vw_hi(g, i)
                if not last:
                    wq_hi(g + 1, 2)
                exps(g, 1)
                vw_hi(g, 5)
                vw_hi(g, 6)
                swap(g, 3, 0)
                swap(g, 3, 1)
                vw_hi(g, 7)
                pt_hi(g, 0, 0)
                if not last:
                    wq_hi(g + 1, 3)
                exps(g, 2)
                pt_hi(g, 0, 1)

            for t in range(C):
                act.wait_ge(sm["w2t_mm"], t + 1)
                copy(WQh[:, :, t * P:(t + 1) * P], bank[:, t, :].rearrange("p (c n) -> p c n", n=P)).then_inc(sm["w2t_hi"], 1)
            for c in range(C):
                act.wait_ge(w1_in[c], 16)
                copy(WOh[:, c, :], WOr[:, c, :]).then_inc(sm["w1_hi"], 1)
            x_hi(0, 0)
            x_hi(1, 1)
            act.wait_ge(sm["b2_in"], 16)
            copy(PTh[0:1, 0, 0:D], QS[0:1, 0, :]).then_inc(sm["b2_hi"], 1)

            def at_hi(s):
                act.wait_ge(sm["at_masked"], s + 1)
                copy(VWh[:, 0, s, :], QA[:, s % 2, :]).then_inc(sm["at_hi"], 1)

            at_hi(0)
            at_hi(1)
            x_hi(2, 2)
            at_hi(2)
            x_hi(3, 3)
            tr_hi(4, CTh[:, 0:2, :])
            at_hi(3)
            tr_hi(5, CTh[:, 2:4, :])
            wq_hi(0, 0)
            wkv_hi(0)
            gelu(0)
            x_hi(6, 4)
            gelu(1)
            x_hi(7, 5)
            wq_hi(0, 1)
            wo_hi(0)
            gelu(2)
            x_hi(8, 6)
            gelu(3)
            x_hi(9, 7)
            wq_hi(0, 2)
            gelu(4)
            x_hi(10, 0)
            wq_hi(0, 3)
            gelu(5)
            x_hi(11, 1)
            gelu(6)
            x_hi(12, 2)
            gelu(7)
            x_hi(13, 3)

            group(0, first=True)
            with act.Fori(1, LAST) as g:
                group(g)

            f_dst = [WQh[:, 0, :], WQh[:, 1, :], WQh[:, 2, :], WQh[:, 3, :], WOh[:, 0, :], WOh[:, 1, :]]

            def f_hi(j):
                act.wait_ge(sm["f_mm"], j + 1)
                copy(f_dst[j], bank[:, F_BANKS[j], :]).then_inc(sm["f_hi"], 1)

            def normalize(k, m):
                act.wait_ge(sm["ln_shift"], 2 * (m + 1))
                for t in (2 * m, 2 * m + 1):
                    act.activation(X[:, t, :], X[:, t, :], ACT.Identity, bias=NM[:, t:t + 1], scale=RS[:, t:t + 1])\
                        .then_inc(sm["ln_out"], 1)

            def router_exp():
                act.wait_ge(sm["lg_step"], 3)
                act.activation(LG[:, 2, :], LG[:, 1, :], ACT.Exp).then_inc(sm["lg_exp"], 1)

            def routed(half):
                act.wait_ge(sm["rt_out"], 1)
                act.wait_ge(sm["tt_mm"], half + 1)
                for j in range(2):
                    m = act.activation(QS[:, half, j * S:(j + 1) * S], bank[:, LORA_BANK + half, j * S:(j + 1) * S],
                                       ACT.Copy, scale=RT[:, 2 * half + j:2 * half + j + 1])
                m.then_inc(sm["ts_out"], 1)
                act.wait_ge(sm["ts_out"], half + 1)
                copy(PTh[:, 0, half * HALF:(half + 1) * HALF], QS[:, half, :]).then_inc(sm["ts_hi"], 1)

            def out_scale(m):
                if m < 3:
                    act.wait_ge(sm["ln_shift"], 8 + 2 * (m + 1))
                else:
                    act.wait_ge(sm["last_shift"], 2)
                for t in ((2 * m, 2 * m + 1) if m < 3 else (7,)):
                    act.activation(X[:, t, :], X[:, t, :], ACT.Identity, bias=NM[:, t:t + 1], scale=RS[:, t:t + 1])\
                        .then_inc(sm["out_done"], 1)

            swap(LAST, 0, 0)
            swap(LAST, 0, 1)
            wo_hi(LAST)
            exps(LAST - 1, 3)
            kv(LAST)
            swap(LAST, 1, 0)
            swap(LAST, 1, 1)
            pt_hi(LAST - 1, 1, 0)
            pt_hi(LAST - 1, 1, 1)
            swap(LAST, 2, 0)
            exps(LAST, 0)
            vw_hi(LAST, 0)
            vw_hi(LAST, 1)
            exps(LAST, 1)
            vw_hi(LAST, 2)
            swap(LAST, 2, 1)
            vw_hi(LAST, 3)
            swap(LAST, 3, 0)
            vw_hi(LAST, 4)
            swap(LAST, 3, 1)
            vw_hi(LAST, 5)
            vw_hi(LAST, 6)
            pt_hi(LAST, 0, 0)
            exps(LAST, 2)
            exps(LAST, 3)
            vw_hi(LAST, 7)
            f_hi(0)
            pt_hi(LAST, 0, 1)
            pt_hi(LAST, 1, 0)
            f_hi(1)
            pt_hi(LAST, 1, 1)
            for i in range(2, 5):
                f_hi(i)
            normalize(1, 0)
            x_hi(18, 0)
            f_hi(5)
            x_hi(19, 1)
            normalize(1, 1)
            x_hi(20, 2)
            x_hi(21, 3)
            normalize(1, 2)
            x_hi(22, 4)
            x_hi(23, 5)
            normalize(1, 3)
            x_hi(24, 6)
            x_hi(25, 7)
            router_exp()
            routed(0)
            routed(1)
            for i in range(0, 4):
                out_scale(i)

        @block.vector
        def _(dve):
            def lo_part(o, i, hi):
                return dve.tensor_tensor(o, i, f32(hi), ALU.subtract)

            def tr_lo(n, hi, lo):
                dve.wait_ge(sm["tr_hi"], n + 1)
                lo_part(lo, bank[:, tr_bank(n), :].rearrange("p (c n) -> p c n", n=lo.shape[-1]), hi)\
                    .then_inc(sm["tr_lo"], 1)

            def x_lo(n, t):
                tr_lo(n, XTh[:, :, t * P:(t + 1) * P], XTl[:, :, t * P:(t + 1) * P])

            def masked(s):
                dve.wait_ge(sm["at_mm"], s + 1)
                dve.tensor_tensor(QA[:, s % 2, :], bank[:, (4, 5, 0, 1)[s], :],
                                  SMASK[:, s, :], ALU.mult).then_inc(sm["at_masked"], 1)
                dve.wait_ge(sm["at_hi"], s + 1)
                lo_part(VWl[:, 0, s, :], QA[:, s % 2, :], VWh[:, 0, s, :]).then_inc(sm["at_lo"], 1)

            def stats(k, t):
                n = NT * k + t
                dve.bn_stats(BST[:, t % 2, :], X[:, t, :]).then_inc(sm["ln_stats"], 1)
                dve.wait_ge(sm["ln_stats"], n + 1)
                dve.bn_aggr(MV[:, t, :], BST[:, t % 2, :]).then_inc(sm["ln_mean"], 1)

            def guess(k, m):
                i = 3 * (4 * k + m)
                v, r = VE[:, 2 * m:2 * m + 2], RS[:, 2 * m:2 * m + 2]
                dve.wait_ge(sm["ln_mean"], NT * k + 2 * m + 2)
                dve.tensor_scalar(v, MV[:, 2 * m:2 * m + 2, 1], LN_EPS, None, ALU.add)
                dve.tensor_scalar(VH[:, 2 * m:2 * m + 2], MV[:, 2 * m:2 * m + 2, 1], LN_EPS, -0.5, ALU.add, ALU.mult)\
                    .then_inc(sm["ln_guess"], 1)
                dve.wait_ge(sm["ln_guess"], i + 1)
                dve.tensor_scalar(r.bitcast(I32), v.bitcast(I32), 1, None, ALU.logical_shift_right)\
                    .then_inc(sm["ln_guess"], 1)
                dve.wait_ge(sm["ln_guess"], i + 2)
                dve.tensor_scalar(r.bitcast(I32), r.bitcast(I32), -1.0, RSQRT_GUESS, ALU.mult, ALU.add)\
                    .then_inc(sm["ln_guess"], 1)

            def newton(k, m):
                dve.wait_ge(sm["ln_guess"], 3 * (4 * k + m + 1))
                i = 4 * NEWTON_STEPS * (4 * k + m)
                dve.wait_ge(sm["ln_newton"], i)
                vh, r, w = ([a[:, t:t + 1] for t in (2 * m, 2 * m + 1)] for a in (VH, RS, NW))
                for _ in range(NEWTON_STEPS):
                    for j in range(2):
                        dve.wait_ge(sm["ln_newton"], i - 1 + j)
                        dve.tensor_scalar(w[j], r[j], r[j], vh[j], ALU.mult, ALU.mult).then_inc(sm["ln_newton"], 1)
                    for j in range(2):
                        dve.wait_ge(sm["ln_newton"], i + 1 + j)
                        dve.tensor_scalar(r[j], w[j], 1.5, r[j], ALU.add, ALU.mult).then_inc(sm["ln_newton"], 1)
                    i += 4

            def normalize(k, m):
                dve.wait_ge(sm["ln_newton"], 4 * NEWTON_STEPS * (4 * k + m + 1))
                for t in (2 * m, 2 * m + 1):
                    dve.tensor_scalar(X[:, t, :], X[:, t, :], MV[:, t, 0:1], RS[:, t:t + 1],
                                      ALU.subtract, ALU.mult).then_inc(sm["ln_out"], 1)

            def residual(t):
                dve.wait_ge(sm["gelu_done"], t + 1)
                dve.tensor_tensor(X[:, t, :], X[:, t, :], SM[:, t % 2, :], ALU.add).then_inc(sm["x_added"], 1)
                dve.wait_ge(sm["x_added"], t + 1)
                stats(0, t)

            def by_pos(table, copies, n):
                return table[:, 0:n].unsqueeze(1).broadcast_to([P, copies, n])

            def kv_cos(g):
                dve.wait_ge(sm["kv_act"], g + 1)
                dve.tensor_tensor(KA[:, :].rearrange("p (b k) -> p b k", b=B),
                                  bank[:, VW_BANK, 0:B * KS].rearrange("p (b k) -> p b k", b=B),
                                  by_pos(COS, B, KS), ALU.mult).then_inc(sm["k_cos"], 1)
                ksw = KSW[:, :].rearrange("p (b k) -> p b k", b=B)
                dve.tensor_tensor(ksw, ksw, by_pos(SIN, B, KS), ALU.mult).then_inc(sm["k_sin"], 1)
                lo_part(VTl[:, :], bank[:, VW_BANK, B * KS:2 * B * KS], VTh[:, :]).then_inc(sm["v_lo"], 1)

            def kv_rot(g):
                dve.wait_ge(sm["k_cos"], g + 1)
                dve.wait_ge(sm["k_sin"], g + 1)
                if counted(G * g):
                    dve.wait_ge(sm["s_mm"], G * g)
                ka, ksw = (a[:, :].rearrange("p (a b k) -> p a b k", a=2, b=2) for a in (KA, KSW))
                dve.tensor_tensor(KR[:, :, 0:2, :], ka, ksw, ALU.add)
                dve.tensor_tensor(KR[:, :, 2, :], ka[:, :, 0, :], ksw[:, :, 0, :], ALU.add).then_inc(sm["k_rot"], 1)

            def q_cos(g, h, half):
                i = 2 * G * g + 2 * h + half
                dve.wait_ge(sm["q_swap"], i + 1)
                dve.tensor_tensor(QA[:, half, :].rearrange("p (b s) -> p b s", b=2),
                                  bank[:, Q_BANK + half, :].rearrange("p (b s) -> p b s", b=2),
                                  by_pos(COS, 2, S), ALU.mult).then_inc(sm["q_cos"], 1)

            def q_rot(g, h, half):
                i = 2 * G * g + 2 * h + half
                dve.wait_ge(sm["q_cos"], i + 1)
                dve.wait_ge(sm["q_sin"], i + 1)
                if half == 0:
                    if counted(G * g + h - 1):
                        dve.wait_ge(sm["s_mm"], G * g + h - 1)
                dve.tensor_tensor(QR[:, h % 2, half * HALF:(half + 1) * HALF], QA[:, half, :], QS[:, half, :],
                                  ALU.add).then_inc(sm["q_rot"], 1)

            def sm_rows(h):
                return SM[:, h % 2, :].rearrange("p (t k) -> p t k", k=KS)

            def mask_scores(g, h):
                i = G * g + h
                dve.wait_ge(sm["s_mm"], i + 1)
                if counted(i - 1):
                    dve.wait_ge(sm["p_done"], i - 1)
                dve.scalar_tensor_tensor(out=sm_rows(h), in0=bank[:, S_BANK:S_BANK + 2, :].rearrange("p a (t k) -> p (a t) k", k=P)[:, :, 0:KS],
                                         scalar=1.0 / math.sqrt(DK), in1=MSK[:, :, :], op0=ALU.mult, op1=ALU.add)\
                    .then_inc(sm["s_masked"], 1)

            def row_max(g, h):
                dve.wait_ge(sm["s_masked"], G * g + h + 1)
                dve.tensor_reduce(MX[:, h % 2, :], sm_rows(h), AX_X, ALU.max).then_inc(sm["s_max"], 1)

            def shift(g, h):
                dve.wait_ge(sm["s_max"], G * g + h + 1)
                dve.tensor_tensor(sm_rows(h), sm_rows(h), MX[:, h % 2, :].unsqueeze(2).broadcast_to([P, NT, KS]),
                                  ALU.subtract).then_inc(sm["s_sub"], 1)

            def row_sum(g, h):
                dve.wait_ge(sm["s_exp"], G * g + h + 1)
                dve.tensor_reduce(SU[:, h % 2, :], sm_rows(h), AX_X, ALU.add).then_inc(sm["s_sum"], 1)

            def row_inverse(g, h):
                dve.wait_ge(sm["s_sum"], G * g + h + 1)
                dve.reciprocal(RI[:, h % 2, :], SU[:, h % 2, :]).then_inc(sm["s_inv"], 1)

            def pt_lo(g, pair, part):
                dve.wait_ge(sm["pt_hi"], 4 * g + 2 * pair + part + 1)
                lo_part(PTl[:, pair, part * HALF:(part + 1) * HALF], bank[:, t_bank(part), :],
                        PTh[:, pair, part * HALF:(part + 1) * HALF]).then_inc(sm["pt_lo"], 1)

            def vw_lo(g, u):
                pair, par, bp = u // 4, u // 2 % 2, u % 2
                dve.wait_ge(sm["vw_hi"], 2 * G * g + u + 1)
                for j in range(2):
                    o = (slice(64 * par, 64 * par + 64), pair, 2 * bp + j, slice(0, D))
                    m = lo_part(VWl[o], bank[64 * j:64 * j + 64, vw_bank(u), :], VWh[o])
                m.then_inc(sm["vw_lo"], 1)

            def accumulate(g, t):
                dve.wait_ge(sm["pv_mm"], NT * g + t + 1)
                dve.tensor_tensor(X[:, t, :], X[:, t, :], bank[:, PV_BANK + t % 2, :], ALU.add)\
                    .then_inc(sm["x_added"], 1)

            def group(g, first=False, last=False):
                if first:
                    for t in range(4, NT):
                        x_lo(10 + t, t)
                    kv_cos(g)
                    kv_rot(g)
                    q_cos(g, 0, 0)
                    q_cos(g, 0, 1)
                    q_rot(g, 0, 0)
                    q_rot(g, 0, 1)
                if not first:
                    row_sum(g - 1, 2)
                    pt_lo(g - 1, 0, 0)
                    pt_lo(g - 1, 0, 1)
                    row_inverse(g - 1, 2)
                    q_cos(g, 0, 0)
                    mask_scores(g - 1, 3)
                    q_cos(g, 0, 1)
                    row_max(g - 1, 3)
                    shift(g - 1, 3)
                    q_rot(g, 0, 0)
                    row_sum(g - 1, 3)
                    row_inverse(g - 1, 3)
                q_cos(g, 1, 0)
                if not first:
                    q_rot(g, 0, 1)
                    kv_cos(g)
                q_cos(g, 1, 1)
                if not first:
                    pt_lo(g - 1, 1, 0)
                    kv_rot(g)
                q_rot(g, 1, 0)
                if not first:
                    accumulate(g - 1, 0)
                    pt_lo(g - 1, 1, 1)
                mask_scores(g, 0)
                if not first:
                    accumulate(g - 1, 1)
                    accumulate(g - 1, 2)
                row_max(g, 0)
                shift(g, 0)
                if not first:
                    accumulate(g - 1, 3)
                    accumulate(g - 1, 4)
                q_cos(g, 2, 0)
                if not first:
                    accumulate(g - 1, 5)
                q_rot(g, 1, 1)
                q_rot(g, 2, 0)
                if not first:
                    accumulate(g - 1, 6)
                    accumulate(g - 1, 7)
                vw_lo(g, 0)
                row_sum(g, 0)
                row_inverse(g, 0)
                vw_lo(g, 1)
                q_cos(g, 2, 1)
                mask_scores(g, 1)
                vw_lo(g, 2)
                vw_lo(g, 3)
                row_max(g, 1)
                q_rot(g, 2, 1)
                shift(g, 1)
                vw_lo(g, 4)
                row_sum(g, 1)
                vw_lo(g, 5)
                row_inverse(g, 1)
                vw_lo(g, 6)
                q_cos(g, 3, 0)
                q_cos(g, 3, 1)
                mask_scores(g, 2)
                row_max(g, 2)
                shift(g, 2)
                q_rot(g, 3, 0)
                vw_lo(g, 7)
                q_rot(g, 3, 1)

            for t in range(C):
                dve.wait_ge(sm["w2t_hi"], t + 1)
                w = slice(t * P, (t + 1) * P)
                lo_part(WQl[:, :, w], bank[:, t, :].rearrange("p (c n) -> p c n", n=P), WQh[:, :, w])\
                    .then_inc(sm["w2t_lo"], 1)
            for c in (0, 2):
                dve.wait_ge(sm["w1_hi"], c + 1)
                lo_part(WOl[:, c, :], WOr[:, c, :], WOh[:, c, :]).then_inc(sm["w1_lo_even"], 1)
            x_lo(0, 0)
            x_lo(1, 1)
            dve.wait_ge(sm["b2_hi"], 1)
            lo_part(PTl[0:1, 0, 0:D], QS[0:1, 0, :], PTh[0:1, 0, 0:D]).then_inc(sm["b2_lo"], 1)
            dve.wait_ge(sm["ones_set"], 1)
            dve.tensor_copy(PTh[0:1, 1, 0:P], KA[0:1, 0:P]).then_inc(sm["b2_lo"], 1)
            dve.wait_ge(sm["mask_in"], 16)
            masked(0)
            masked(1)
            x_lo(2, 2)
            masked(2)
            x_lo(3, 3)
            tr_lo(4, CTh[:, 0:2, :], CTl[:, 0:2, :])
            masked(3)
            tr_lo(5, CTh[:, 2:4, :], CTl[:, 2:4, :])
            x_lo(6, 4)
            residual(0)
            x_lo(7, 5)
            residual(1)
            guess(0, 0)
            x_lo(8, 6)
            residual(2)
            x_lo(9, 7)
            normalize(0, 0)
            residual(3)
            guess(0, 1)
            residual(4)
            x_lo(10, 0)
            normalize(0, 1)
            residual(5)
            guess(0, 2)
            x_lo(11, 1)
            residual(6)
            x_lo(12, 2)
            normalize(0, 2)
            x_lo(13, 3)
            residual(7)
            guess(0, 3)
            newton(0, 3)
            normalize(0, 3)
            dve.wait_ge(sm["rope_in"], 32)
            dve.wait_ge(sm["amask_in"], 16)

            group(0, first=True)
            with dve.Fori(1, LAST) as g:
                group(g)

            f_h = [WQh[:, 0, :], WQh[:, 1, :], WQh[:, 2, :], WQh[:, 3, :], WOh[:, 0, :], WOh[:, 1, :]]
            f_l = [WQl[:, 0, :], WQl[:, 1, :], WQl[:, 2, :], WQl[:, 3, :], WOl[:, 0, :], WOl[:, 1, :]]

            def f_lo(j):
                if j < 6:
                    dve.wait_ge(sm["f_hi"], j + 1)
                    m = lo_part(f_l[j], bank[:, F_BANKS[j], :], f_h[j])
                else:
                    dve.wait_ge(sm["f_mm"], 7)
                    m = dve.tensor_copy(RWT[:, :, :].rearrange("p c e -> p (c e)"), bank[:, F_BANKS[j], 0:C * E])
                m.then_inc(sm["f_lo"], 1)

            def x2_stats(t):
                dve.wait_ge(sm["x_added"], NT + NT * LAST + t + 1)
                stats(1, t)

            def x2_lo(t):
                a, b = ((ROUTE_FROM, P), (0, P + ROUTE_END))[t % 2]
                dve.wait_ge(sm["tr_hi"], 18 + t + 1)
                dve.tensor_reduce(TS[:, t, :], bank[:, tr_bank(18 + t), :].rearrange("p (c n) -> p c n", n=P)[:, :, a:b],
                                  AX_X, ALU.add).then_inc(sm["tile_sum"], 1)
                x_lo(18 + t, t)

            def mean_tokens():
                dve.wait_ge(sm["tile_sum"], NT)
                ts = TS[:, :, :].rearrange("p (b i) c -> p i c b", i=TPB)
                dve.tensor_tensor(QT[:, :, :], ts[:, 0, :, :], ts[:, 1, :, :], ALU.add).then_inc(sm["mean_out"], 1)

            def router_shift():
                dve.wait_ge(sm["lg_mm"], 1)
                dve.wait_ge(sm["rb_in"], 16)
                dve.scalar_tensor_tensor(out=LG[:, 0, :], in0=bank[0:B, LG_BANK, 0:E], scalar=1.0 / (S + ROUTE_END - ROUTE_FROM),
                                         in1=RB[:, :], op0=ALU.mult, op1=ALU.add).then_inc(sm["lg_step"], 1)
                dve.wait_ge(sm["lg_step"], 1)
                dve.tensor_reduce(LS[:, 0:1], LG[:, 0, :], AX_X, ALU.max).then_inc(sm["lg_step"], 1)
                dve.wait_ge(sm["lg_step"], 2)
                dve.tensor_scalar(LG[:, 1, :], LG[:, 0, :], LS[:, 0:1], None, ALU.subtract).then_inc(sm["lg_step"], 1)

            def router_probs():
                dve.wait_ge(sm["lg_exp"], 1)
                dve.tensor_reduce(LS[:, 1:2], LG[:, 2, :], AX_X, ALU.add).then_inc(sm["lg_step"], 1)
                dve.wait_ge(sm["lg_step"], 4)
                dve.reciprocal(LS[:, 2:3], LS[:, 1:2]).then_inc(sm["lg_step"], 1)
                dve.wait_ge(sm["lg_step"], 5)
                dve.tensor_scalar(R2[:, :].rearrange("p (e r) -> p e r", e=E),
                                  LG[:, 2, :].unsqueeze(2).broadcast_to([B, E, R]), LS[:, 2:3], LORA_SCALING,
                                  ALU.mult, ALU.mult).then_inc(sm["r_out"], 1)

            def route_out():
                dve.wait_ge(sm["rt_mm"], 1)
                dve.tensor_copy(RT[:, :], bank[:, RT_BANK, 0:B]).then_inc(sm["rt_out"], 1)

            def routed_lo(half):
                dve.wait_ge(sm["ts_hi"], half + 1)
                lo_part(PTl[:, 0, half * HALF:(half + 1) * HALF], QS[:, half, :],
                        PTh[:, 0, half * HALF:(half + 1) * HALF]).then_inc(sm["ts_lo"], 1)

            def out_add(t):
                dve.wait_ge(sm["fy_mm"], t + 1)
                dve.wait_ge(sm["bias_in"], t + 1)
                dve.tensor_tensor(X[:, t, :], X[:, t, :], bank[:, fy_bank(t), :], ALU.add).then_inc(sm["fy_out"], 1)

            def out_stats(t):
                dve.wait_ge(sm["fy_out"], t + 1)
                stats(2, t)

            def out_last():
                newton(2, 3)
                dve.wait_ge(sm["ln_newton"], 4 * NEWTON_STEPS * (4 * 2 + 4))
                dve.tensor_scalar(NM[:, 6:8], MV[:, 6:8, 0], -1.0, None, ALU.mult).then_inc(sm["last_shift"], 1)
                dve.wait_ge(sm["last_shift"], 1)
                dve.tensor_tensor(NM[:, 6:8], NM[:, 6:8], RS[:, 6:8], ALU.mult).then_inc(sm["last_shift"], 1)
                dve.tensor_scalar(X[:, 6, :], X[:, 6, :], MV[:, 6, 0:1], RS[:, 6:7],
                                  ALU.subtract, ALU.mult).then_inc(sm["out_even"], 1)

            q_cos(LAST, 0, 0)
            pt_lo(LAST - 1, 0, 0)
            row_sum(LAST - 1, 2)
            mask_scores(LAST - 1, 3)
            row_max(LAST - 1, 3)
            shift(LAST - 1, 3)
            q_cos(LAST, 0, 1)
            row_sum(LAST - 1, 3)
            row_inverse(LAST - 1, 2)
            q_rot(LAST, 0, 0)
            row_inverse(LAST - 1, 3)
            pt_lo(LAST - 1, 0, 1)
            q_cos(LAST, 1, 0)
            q_rot(LAST, 0, 1)
            kv_cos(LAST)
            kv_rot(LAST)
            q_cos(LAST, 1, 1)
            pt_lo(LAST - 1, 1, 0)
            pt_lo(LAST - 1, 1, 1)
            q_rot(LAST, 1, 0)
            mask_scores(LAST, 0)
            accumulate(LAST - 1, 0)
            q_rot(LAST, 1, 1)
            accumulate(LAST - 1, 1)
            accumulate(LAST - 1, 2)
            q_cos(LAST, 2, 0)
            accumulate(LAST - 1, 3)
            row_max(LAST, 0)
            mask_scores(LAST, 1)
            q_rot(LAST, 2, 0)
            accumulate(LAST - 1, 4)
            shift(LAST, 0)
            accumulate(LAST - 1, 5)
            row_sum(LAST, 0)
            accumulate(LAST - 1, 6)
            row_max(LAST, 1)
            row_inverse(LAST, 0)
            shift(LAST, 1)
            vw_lo(LAST, 0)
            vw_lo(LAST, 1)
            accumulate(LAST - 1, 7)
            row_sum(LAST, 1)
            vw_lo(LAST, 2)
            row_inverse(LAST, 1)
            q_cos(LAST, 2, 1)
            vw_lo(LAST, 3)
            q_cos(LAST, 3, 0)
            q_rot(LAST, 2, 1)
            vw_lo(LAST, 4)
            q_rot(LAST, 3, 0)
            q_cos(LAST, 3, 1)
            mask_scores(LAST, 2)
            q_rot(LAST, 3, 1)
            row_max(LAST, 2)
            vw_lo(LAST, 5)
            vw_lo(LAST, 6)
            mask_scores(LAST, 3)
            shift(LAST, 2)
            row_max(LAST, 3)
            shift(LAST, 3)
            row_sum(LAST, 2)
            row_inverse(LAST, 2)
            row_sum(LAST, 3)
            row_inverse(LAST, 3)
            pt_lo(LAST, 0, 0)
            f_lo(0)
            pt_lo(LAST, 0, 1)
            vw_lo(LAST, 7)
            pt_lo(LAST, 1, 0)
            f_lo(1)
            pt_lo(LAST, 1, 1)
            f_lo(2)
            accumulate(LAST, 0)
            f_lo(3)
            accumulate(LAST, 1)
            x2_stats(0)
            x2_stats(1)
            accumulate(LAST, 2)
            guess(1, 0)
            accumulate(LAST, 3)
            x2_stats(2)
            accumulate(LAST, 4)
            x2_stats(3)
            x2_stats(4)
            guess(1, 1)
            accumulate(LAST, 5)
            f_lo(4)
            x2_stats(5)
            x2_lo(0)
            accumulate(LAST, 6)
            guess(1, 2)
            f_lo(5)
            x2_lo(1)
            accumulate(LAST, 7)
            x2_stats(6)
            x2_stats(7)
            x2_lo(2)
            guess(1, 3)
            for i in range(3, 8):
                x2_lo(i)
            f_lo(6)
            mean_tokens()
            router_shift()
            router_probs()
            route_out()
            routed_lo(0)
            out_add(0)
            out_add(1)
            out_stats(0)
            out_stats(1)
            out_add(2)
            guess(2, 0)
            routed_lo(1)
            out_add(3)
            out_stats(2)
            out_stats(3)
            guess(2, 1)
            out_add(4)
            out_add(5)
            out_stats(4)
            out_stats(5)
            guess(2, 2)
            out_add(6)
            out_add(7)
            out_stats(6)
            out_stats(7)
            guess(2, 3)
            out_last()

        @block.gpsimd
        def _(pool):
            def wq_lo(g, h):
                pool.wait_ge(sm["wq_hi"], G * g + h + 1)
                w = slice(h * DK, (h + 1) * DK)
                pool.tensor_tensor(WQl[:, :, w], WQr[:, :, w], f32(WQh[:, :, w]), ALU.subtract)\
                    .then_inc(sm["wq_lo"], 1)

            def wkv_lo(g, i):
                pool.wait_ge(sm["wkv_hi"], g + 1)
                pool.tensor_tensor(KVl[:, i, :, :], KVr[:, i, :, :], f32(KVh[:, i, :, :]), ALU.subtract)\
                    .then_inc(sm["wkv_lo"], 1)

            def wo_lo(g, h):
                pool.wait_ge(sm["wo_hi"], G * g + h + 1)
                pool.tensor_tensor(WOl[:, h, :], WOr[:, h, :], f32(WOh[:, h, :]), ALU.subtract)\
                    .then_inc(sm["wo_lo"], 1)

            def newton(k, m):
                pool.wait_ge(sm["ln_guess"], 3 * (4 * k + m + 1))
                i = 4 * NEWTON_STEPS * (4 * k + m)
                vh, r, w = (a[:, 2 * m:2 * m + 2] for a in (VH, RS, NW))
                for _ in range(NEWTON_STEPS):
                    pool.tensor_tensor(w, r, r, ALU.mult).then_inc(sm["ln_newton"], 1)
                    pool.wait_ge(sm["ln_newton"], i + 1)
                    pool.tensor_tensor(w, w, vh, ALU.mult).then_inc(sm["ln_newton"], 1)
                    pool.wait_ge(sm["ln_newton"], i + 2)
                    pool.tensor_scalar(w, w, 1.5, None, ALU.add).then_inc(sm["ln_newton"], 1)
                    pool.wait_ge(sm["ln_newton"], i + 3)
                    pool.tensor_tensor(r, r, w, ALU.mult).then_inc(sm["ln_newton"], 1)
                    pool.wait_ge(sm["ln_newton"], i + 4)
                    i += 4

            def q_sin(g, h, half):
                pool.wait_ge(sm["q_swap"], 2 * G * g + 2 * h + half + 1)
                q = QS[:, half, :].rearrange("p (b s) -> p b s", b=2)
                pool.tensor_tensor(q, q, SIN[:, :].unsqueeze(1).broadcast_to([P, 2, S]), ALU.mult)\
                    .then_inc(sm["q_sin"], 1)

            def probs(g, h):
                pool.wait_ge(sm["s_inv"], G * g + h + 1)
                if h == 0:
                    if counted(4 * (g - 1) + 2):
                        pool.wait_ge(sm["t_mm"], 4 * (g - 1) + 2)
                if h == 2 and isinstance(g, int):
                    pool.wait_ge(sm["t_mm"], 4 * g)
                elif h == 2:
                    pool.wait_ge(sm["t_mm"], 4 * g + 1)
                pool.tensor_tensor(PB[:, h // 2, :, h % 2, :], SM[:, h % 2, :].rearrange("p (t k) -> p t k", k=KS),
                                   RI[:, h % 2, :].unsqueeze(2).broadcast_to([P, NT, KS]), ALU.mult)\
                    .then_inc(sm["p_done"], 1)

            def group(g, first=False, last=False):
                if not first:
                    wo_lo(g, 0)
                q_sin(g, 0, 0)
                if not first:
                    probs(g - 1, 2)
                q_sin(g, 0, 1)
                if not first:
                    probs(g - 1, 3)
                if not last:
                    wq_lo(g + 1, 0)
                q_sin(g, 1, 0)
                if not last:
                    wkv_lo(g + 1, 0)
                if not first:
                    wo_lo(g, 1)
                if not first:
                    wo_lo(g, 2)
                q_sin(g, 1, 1)
                q_sin(g, 2, 0)
                if not first:
                    wo_lo(g, 3)
                probs(g, 0)
                if not last:
                    wq_lo(g + 1, 1)
                q_sin(g, 2, 1)
                probs(g, 1)
                if not last:
                    wq_lo(g + 1, 2)
                q_sin(g, 3, 0)
                q_sin(g, 3, 1)
                if not last:
                    wq_lo(g + 1, 3)
                    wkv_lo(g + 1, 1)

            pool.memset(ID[:, :], 0.0).then_inc(sm["ident"], 1)
            pool.wait_ge(sm["ident"], 1)
            pool.affine_select(out=ID[:, :], in_=ID[:, :], compare_op=ALU.not_equal, fill=1.0, base=0,
                               pattern=[[-1, P]], channel_multiplier=1).then_inc(sm["ident"], 1)
            pool.memset(KA[0:1, 0:P], 1.0).then_inc(sm["ones_set"], 1)
            for c in (1, 3):
                pool.wait_ge(sm["w1_hi"], c + 1)
                pool.tensor_tensor(WOl[:, c, :], WOr[:, c, :], f32(WOh[:, c, :]), ALU.subtract)\
                    .then_inc(sm["w1_lo_odd"], 1)
            wq_lo(0, 0)
            wkv_lo(0, 0)
            wkv_lo(0, 1)
            wq_lo(0, 1)
            newton(0, 0)
            wo_lo(0, 0)
            wo_lo(0, 1)
            newton(0, 1)
            wo_lo(0, 2)
            wo_lo(0, 3)
            newton(0, 2)
            wq_lo(0, 2)
            wq_lo(0, 3)
            pool.wait_ge(sm["rope_in"], 32)

            group(0, first=True)
            with pool.Fori(1, LAST) as g:
                group(g)

            def mean_shift(k, m):
                pair = slice(2 * m, 2 * m + 2)
                pool.wait_ge(sm["ln_newton"], 4 * NEWTON_STEPS * (4 * k + m + 1))
                pool.tensor_tensor(NM[:, pair], MV[:, pair, 0], RS[:, pair], ALU.mult).then_inc(sm["ln_shift"], 1)
                pool.wait_ge(sm["ln_shift"], 8 * (k - 1) + 2 * m + 1)
                pool.tensor_scalar(NM[:, pair], NM[:, pair], -1.0, None, ALU.mult).then_inc(sm["ln_shift"], 1)

            def add_bias(t):
                pool.wait_ge(sm["fb_in"], 16)
                pool.wait_ge(sm["tr_mm"], 18 + t + 1)
                pool.tensor_tensor(X[:, t, :], X[:, t, :], WOr[:, 3, :], ALU.add).then_inc(sm["bias_in"], 1)

            def out_shift(m):
                newton(2, m)
                mean_shift(2, m)

            wo_lo(LAST, 0)
            q_sin(LAST, 0, 0)
            q_sin(LAST, 0, 1)
            probs(LAST - 1, 2)
            probs(LAST - 1, 3)
            wo_lo(LAST, 1)
            q_sin(LAST, 1, 0)
            q_sin(LAST, 1, 1)
            q_sin(LAST, 2, 0)
            wo_lo(LAST, 2)
            probs(LAST, 0)
            wo_lo(LAST, 3)
            q_sin(LAST, 2, 1)
            probs(LAST, 1)
            q_sin(LAST, 3, 0)
            q_sin(LAST, 3, 1)
            probs(LAST, 2)
            probs(LAST, 3)
            newton(1, 0)
            mean_shift(1, 0)
            newton(1, 1)
            mean_shift(1, 1)
            add_bias(0)
            newton(1, 2)
            mean_shift(1, 2)
            add_bias(1)
            newton(1, 3)
            mean_shift(1, 3)
            for i in range(2, 8):
                add_bias(i)
            for i in range(0, 3):
                out_shift(i)


_INS = ['x', 'ctx_4096', 'mask_BxSxS2_ff0', 'L0_attn_w1', 'L0_attn_w2', 'L0_attn_b2', 'L0_attn_sparse_mask', 'L0_xattn_wq', 'L0_xattn_wk',
        'L0_xattn_wv', 'L0_xattn_wo', 'L0_ffn_W', 'L0_ffn_b', 'L0_ffn_A', 'L0_ffn_B', 'L0_ffn_router_W', 'L0_ffn_router_b']


def kernel(**inputs):
    import numpy as _np
    import concourse.bacc as _bacc
    from concourse import mybir as _mybir
    from concourse.bass_utils import run_bass_kernel_spmd as _run

    nc = _bacc.Bacc("TRN2", target_bir_lowering=False, num_devices=1)
    b, s, d = inputs["x"].shape
    arrays, args = {}, []
    given = [(n, inputs[n]) for n in _INS] + [("rope", rope_tables(P, s))]
    for name, a in given:
        a = _np.ascontiguousarray(a)
        arrays[f"in_{name}_dram"] = a
        args.append(nc.dram_tensor(f"in_{name}_dram", a.shape, _mybir.dt.from_np(a.dtype), kind="ExternalInput").ap())
    args.append(nc.dram_tensor("out_0_dram", (b, s, d), F32, kind="ExternalOutput").ap())
    decoder_layer(nc, *args)
    r = _run(nc, [arrays], core_ids=[0])
    return r.results[0]["out_0_dram"]
```
